# Optimizing a Trainium2 kernel written in Bass

```python
import numpy as np
import jax
import jax.numpy as jnp

def _softmax(x, axis=-1):
    return jax.nn.softmax(x, axis=axis)

def _gelu(x):
    return jax.nn.gelu(x, approximate=True)

def _silu(x):
    return jax.nn.silu(x)

def _sigmoid(x):
    return jax.nn.sigmoid(x)

def _layernorm(x, axis=-1, eps=1e-05):
    m = jnp.mean(x, axis=axis, keepdims=True)
    v = jnp.var(x, axis=axis, keepdims=True)
    return (x - m) / jnp.sqrt(v + eps)

def _scatter_add(tgt, idx, src, axis=0):
    return tgt.at[idx].add(src)

def _segment_sum(src, seg, n):
    return jax.ops.segment_sum(src, seg, n)
kernel_name = 'mk_dlrm_tower_d1_rec_r8_baf877'

def setup_inputs(seed: int=0):
    np.random.seed(seed)
    _w = jnp.asarray

    def _rec_inputs():
        import jax
        import jax.numpy as jnp
        _tk = jax.random.key(seed)
        dense_ctx = jax.random.normal(jax.random.fold_in(_tk, 190), (512, 16), jnp.float32)
        ids = jnp.stack([jax.random.randint(jax.random.fold_in(_tk, 200 + f), (512,), 0, v, jnp.int32) for f, v in enumerate([1000, 12500, 1000, 12500, 12500, 12500, 125000, 1250, 125000, 12500, 1250, 12500, 125000, 12500, 1000, 125000, 125000, 1000, 1250, 1250, 125000, 1000, 125000, 12500, 125000, 12500, 1250, 12500, 12500, 1000, 1000, 12500, 125000, 1000, 1000, 12500, 1250, 12500, 125000])], axis=1)
        tbl_0 = 0.05 * jax.random.normal(jax.random.fold_in(_tk, 500 + 0), (1000, 16), jnp.float32)
        tbl_1 = 0.05 * jax.random.normal(jax.random.fold_in(_tk, 500 + 1), (12500, 16), jnp.float32)
        tbl_2 = 0.05 * jax.random.normal(jax.random.fold_in(_tk, 500 + 2), (1000, 16), jnp.float32)
        tbl_3 = 0.05 * jax.random.normal(jax.random.fold_in(_tk, 500 + 3), (12500, 16), jnp.float32)
        tbl_4 = 0.05 * jax.random.normal(jax.random.fold_in(_tk, 500 + 4), (12500, 16), jnp.float32)
        tbl_5 = 0.05 * jax.random.normal(jax.random.fold_in(_tk, 500 + 5), (12500, 16), jnp.float32)
        tbl_6 = 0.05 * jax.random.normal(jax.random.fold_in(_tk, 500 + 6), (125000, 16), jnp.float32)
        tbl_7 = 0.05 * jax.random.normal(jax.random.fold_in(_tk, 500 + 7), (1250, 16), jnp.float32)
        tbl_8 = 0.05 * jax.random.normal(jax.random.fold_in(_tk, 500 + 8), (125000, 16), jnp.float32)
        tbl_9 = 0.05 * jax.random.normal(jax.random.fold_in(_tk, 500 + 9), (12500, 16), jnp.float32)
        tbl_10 = 0.05 * jax.random.normal(jax.random.fold_in(_tk, 500 + 10), (1250, 16), jnp.float32)
        tbl_11 = 0.05 * jax.random.normal(jax.random.fold_in(_tk, 500 + 11), (12500, 16), jnp.float32)
        tbl_12 = 0.05 * jax.random.normal(jax.random.fold_in(_tk, 500 + 12), (125000, 16), jnp.float32)
        tbl_13 = 0.05 * jax.random.normal(jax.random.fold_in(_tk, 500 + 13), (12500, 16), jnp.float32)
        tbl_14 = 0.05 * jax.random.normal(jax.random.fold_in(_tk, 500 + 14), (1000, 16), jnp.float32)
        tbl_15 = 0.05 * jax.random.normal(jax.random.fold_in(_tk, 500 + 15), (125000, 16), jnp.float32)
        tbl_16 = 0.05 * jax.random.normal(jax.random.fold_in(_tk, 500 + 16), (125000, 16), jnp.float32)
        tbl_17 = 0.05 * jax.random.normal(jax.random.fold_in(_tk, 500 + 17), (1000, 16), jnp.float32)
        tbl_18 = 0.05 * jax.random.normal(jax.random.fold_in(_tk, 500 + 18), (1250, 16), jnp.float32)
        tbl_19 = 0.05 * jax.random.normal(jax.random.fold_in(_tk, 500 + 19), (1250, 16), jnp.float32)
        tbl_20 = 0.05 * jax.random.normal(jax.random.fold_in(_tk, 500 + 20), (125000, 16), jnp.float32)
        tbl_21 = 0.05 * jax.random.normal(jax.random.fold_in(_tk, 500 + 21), (1000, 16), jnp.float32)
        tbl_22 = 0.05 * jax.random.normal(jax.random.fold_in(_tk, 500 + 22), (125000, 16), jnp.float32)
        tbl_23 = 0.05 * jax.random.normal(jax.random.fold_in(_tk, 500 + 23), (12500, 16), jnp.float32)
        tbl_24 = 0.05 * jax.random.normal(jax.random.fold_in(_tk, 500 + 24), (125000, 16), jnp.float32)
        tbl_25 = 0.05 * jax.random.normal(jax.random.fold_in(_tk, 500 + 25), (12500, 16), jnp.float32)
        tbl_26 = 0.05 * jax.random.normal(jax.random.fold_in(_tk, 500 + 26), (1250, 16), jnp.float32)
        tbl_27 = 0.05 * jax.random.normal(jax.random.fold_in(_tk, 500 + 27), (12500, 16), jnp.float32)
        tbl_28 = 0.05 * jax.random.normal(jax.random.fold_in(_tk, 500 + 28), (12500, 16), jnp.float32)
        tbl_29 = 0.05 * jax.random.normal(jax.random.fold_in(_tk, 500 + 29), (1000, 16), jnp.float32)
        tbl_30 = 0.05 * jax.random.normal(jax.random.fold_in(_tk, 500 + 30), (1000, 16), jnp.float32)
        tbl_31 = 0.05 * jax.random.normal(jax.random.fold_in(_tk, 500 + 31), (12500, 16), jnp.float32)
        tbl_32 = 0.05 * jax.random.normal(jax.random.fold_in(_tk, 500 + 32), (125000, 16), jnp.float32)
        tbl_33 = 0.05 * jax.random.normal(jax.random.fold_in(_tk, 500 + 33), (1000, 16), jnp.float32)
        tbl_34 = 0.05 * jax.random.normal(jax.random.fold_in(_tk, 500 + 34), (1000, 16), jnp.float32)
        tbl_35 = 0.05 * jax.random.normal(jax.random.fold_in(_tk, 500 + 35), (12500, 16), jnp.float32)
        tbl_36 = 0.05 * jax.random.normal(jax.random.fold_in(_tk, 500 + 36), (1250, 16), jnp.float32)
        tbl_37 = 0.05 * jax.random.normal(jax.random.fold_in(_tk, 500 + 37), (12500, 16), jnp.float32)
        tbl_38 = 0.05 * jax.random.normal(jax.random.fold_in(_tk, 500 + 38), (125000, 16), jnp.float32)
        _rk = jax.random.fold_in(_tk, 7)
        W_top1 = 0.0606339 * jax.random.normal(jax.random.fold_in(_tk, 801), (272, 512), jnp.float32)
        W_top2 = 0.0441942 * jax.random.normal(jax.random.fold_in(_tk, 802), (512, 256), jnp.float32)
        W_top3 = 0.0625 * jax.random.normal(jax.random.fold_in(_tk, 803), (256, 1), jnp.float32)
        b_top1 = jnp.zeros((512,), jnp.float32)
        b_top2 = jnp.zeros((256,), jnp.float32)
        return (dense_ctx, ids, tbl_0, tbl_1, tbl_2, tbl_3, tbl_4, tbl_5, tbl_6, tbl_7, tbl_8, tbl_9, tbl_10, tbl_11, tbl_12, tbl_13, tbl_14, tbl_15, tbl_16, tbl_17, tbl_18, tbl_19, tbl_20, tbl_21, tbl_22, tbl_23, tbl_24, tbl_25, tbl_26, tbl_27, tbl_28, tbl_29, tbl_30, tbl_31, tbl_32, tbl_33, tbl_34, tbl_35, tbl_36, tbl_37, tbl_38, W_top1, b_top1, W_top2, b_top2, W_top3)
    dense_ctx, ids, tbl_0, tbl_1, tbl_2, tbl_3, tbl_4, tbl_5, tbl_6, tbl_7, tbl_8, tbl_9, tbl_10, tbl_11, tbl_12, tbl_13, tbl_14, tbl_15, tbl_16, tbl_17, tbl_18, tbl_19, tbl_20, tbl_21, tbl_22, tbl_23, tbl_24, tbl_25, tbl_26, tbl_27, tbl_28, tbl_29, tbl_30, tbl_31, tbl_32, tbl_33, tbl_34, tbl_35, tbl_36, tbl_37, tbl_38, W_top1, b_top1, W_top2, b_top2, W_top3 = _rec_inputs()

    def _L0_rec_setup():
        import jax, jax.numpy as jnp
        import numpy as np
        B, M0, D = (256, 39, 16)
        CIN_SIZE = [128, 128]

        def _cin(inputs, weights):
            X0 = inputs
            Xi = inputs
            res = []
            for W in weights:
                mi = Xi.shape[1]
                z = jnp.einsum('bmd,bnd->bdmn', X0, Xi)
                z = z.reshape(z.shape[0], z.shape[1], M0 * mi)
                Xi = jnp.einsum('bdp,po->bod', z, W)
                res.append(Xi)
            res = jnp.concatenate(res, axis=1)
            return jnp.sum(res, axis=-1)
        key = jax.random.key(seed)
        k1, k2, k3 = jax.random.split(key, 3)
        inputs = jax.random.normal(k1, (B, M0, D), dtype=jnp.float32)
        W0 = jax.random.normal(k2, (M0 * M0, CIN_SIZE[0]), dtype=jnp.float32) * 0.05
        W1 = jax.random.normal(k3, (M0 * CIN_SIZE[0], CIN_SIZE[1]), dtype=jnp.float32) * 0.05
        return {'inputs': inputs, 'W0': W0, 'W1': W1}
    _L0_rec_all = _L0_rec_setup()
    _L0_rec_in = {k: v for k, v in _L0_rec_all.items() if k in ('W0', 'W1')}
    del _L0_rec_all
    return {'dense_ctx': dense_ctx, 'ids': ids, 'tbl_0': tbl_0, 'tbl_1': tbl_1, 'tbl_2': tbl_2, 'tbl_3': tbl_3, 'tbl_4': tbl_4, 'tbl_5': tbl_5, 'tbl_6': tbl_6, 'tbl_7': tbl_7, 'tbl_8': tbl_8, 'tbl_9': tbl_9, 'tbl_10': tbl_10, 'tbl_11': tbl_11, 'tbl_12': tbl_12, 'tbl_13': tbl_13, 'tbl_14': tbl_14, 'tbl_15': tbl_15, 'tbl_16': tbl_16, 'tbl_17': tbl_17, 'tbl_18': tbl_18, 'tbl_19': tbl_19, 'tbl_20': tbl_20, 'tbl_21': tbl_21, 'tbl_22': tbl_22, 'tbl_23': tbl_23, 'tbl_24': tbl_24, 'tbl_25': tbl_25, 'tbl_26': tbl_26, 'tbl_27': tbl_27, 'tbl_28': tbl_28, 'tbl_29': tbl_29, 'tbl_30': tbl_30, 'tbl_31': tbl_31, 'tbl_32': tbl_32, 'tbl_33': tbl_33, 'tbl_34': tbl_34, 'tbl_35': tbl_35, 'tbl_36': tbl_36, 'tbl_37': tbl_37, 'tbl_38': tbl_38, 'W_top1': W_top1, 'b_top1': b_top1, 'W_top2': W_top2, 'b_top2': b_top2, 'W_top3': W_top3, 'L0_rec_W0': _L0_rec_in['W0'], 'L0_rec_W1': _L0_rec_in['W1']}

def reference(dense_ctx, ids, tbl_0, tbl_1, tbl_2, tbl_3, tbl_4, tbl_5, tbl_6, tbl_7, tbl_8, tbl_9, tbl_10, tbl_11, tbl_12, tbl_13, tbl_14, tbl_15, tbl_16, tbl_17, tbl_18, tbl_19, tbl_20, tbl_21, tbl_22, tbl_23, tbl_24, tbl_25, tbl_26, tbl_27, tbl_28, tbl_29, tbl_30, tbl_31, tbl_32, tbl_33, tbl_34, tbl_35, tbl_36, tbl_37, tbl_38, W_top1, b_top1, W_top2, b_top2, W_top3, L0_rec_W0, L0_rec_W1):
    import jax
    import jax.numpy as jnp

    def _L0_rec_ref(inputs, W0, W1):
        import jax, jax.numpy as jnp
        import numpy as np
        B, M0, D = (256, 39, 16)
        CIN_SIZE = [128, 128]

        def _cin(inputs, weights):
            X0 = inputs
            Xi = inputs
            res = []
            for W in weights:
                mi = Xi.shape[1]
                z = jnp.einsum('bmd,bnd->bdmn', X0, Xi)
                z = z.reshape(z.shape[0], z.shape[1], M0 * mi)
                Xi = jnp.einsum('bdp,po->bod', z, W)
                res.append(Xi)
            res = jnp.concatenate(res, axis=1)
            return jnp.sum(res, axis=-1)
        return _cin(inputs, [W0, W1])
    e = jnp.stack([tbl_0[ids[:, 0]], tbl_1[ids[:, 1]], tbl_2[ids[:, 2]], tbl_3[ids[:, 3]], tbl_4[ids[:, 4]], tbl_5[ids[:, 5]], tbl_6[ids[:, 6]], tbl_7[ids[:, 7]], tbl_8[ids[:, 8]], tbl_9[ids[:, 9]], tbl_10[ids[:, 10]], tbl_11[ids[:, 11]], tbl_12[ids[:, 12]], tbl_13[ids[:, 13]], tbl_14[ids[:, 14]], tbl_15[ids[:, 15]], tbl_16[ids[:, 16]], tbl_17[ids[:, 17]], tbl_18[ids[:, 18]], tbl_19[ids[:, 19]], tbl_20[ids[:, 20]], tbl_21[ids[:, 21]], tbl_22[ids[:, 22]], tbl_23[ids[:, 23]], tbl_24[ids[:, 24]], tbl_25[ids[:, 25]], tbl_26[ids[:, 26]], tbl_27[ids[:, 27]], tbl_28[ids[:, 28]], tbl_29[ids[:, 29]], tbl_30[ids[:, 30]], tbl_31[ids[:, 31]], tbl_32[ids[:, 32]], tbl_33[ids[:, 33]], tbl_34[ids[:, 34]], tbl_35[ids[:, 35]], tbl_36[ids[:, 36]], tbl_37[ids[:, 37]], tbl_38[ids[:, 38]]], axis=1)
    z = _L0_rec_ref(e, L0_rec_W0, L0_rec_W1)
    z = z.reshape(z.shape[0], -1)
    h = jnp.concatenate([z, dense_ctx], axis=1)
    h = jnp.maximum(h @ W_top1 + b_top1, 0.0)
    h = jnp.maximum(h @ W_top2 + b_top2, 0.0)
    y = h @ W_top3
    return y

_drawn_inputs = setup_inputs


def setup_inputs(seed=0):
    import zlib

    import numpy as np

    out = dict(_drawn_inputs(seed))
    spreads = {'b_top1': (0.0, 0.1), 'b_top2': (0.0, 0.1)}
    factors = {'tbl_0': 4.623,
     'tbl_1': 5.416,
     'tbl_2': 4.844,
     'tbl_3': 5.318,
     'tbl_4': 5.069,
     'tbl_5': 5.084,
     'tbl_6': 4.883,
     'tbl_7': 5.238,
     'tbl_8': 5.238,
     'tbl_9': 4.867,
     'tbl_10': 5.314,
     'tbl_11': 4.974,
     'tbl_12': 4.823,
     'tbl_13': 4.551,
     'tbl_14': 5.002,
     'tbl_15': 5.007,
     'tbl_16': 5.596,
     'tbl_17': 4.785,
     'tbl_18': 5.151,
     'tbl_19': 5.555,
     'tbl_20': 5.115,
     'tbl_21': 5.137,
     'tbl_22': 4.938,
     'tbl_23': 5.149,
     'tbl_24': 4.925,
     'tbl_25': 4.776,
     'tbl_26': 5.28,
     'tbl_27': 4.888,
     'tbl_28': 4.895,
     'tbl_29': 4.771,
     'tbl_30': 5.103,
     'tbl_31': 4.653,
     'tbl_32': 5.0,
     'tbl_33': 4.863,
     'tbl_34': 4.958,
     'tbl_35': 4.805,
     'tbl_36': 5.156,
     'tbl_37': 5.046,
     'tbl_38': 5.366,
     'L0_rec_W1': 5.656}
    for name, (base, spread) in spreads.items():
        noise = np.random.default_rng([zlib.crc32(name.encode()), seed]).standard_normal(out[name].shape)
        drawn = base * np.exp(spread * noise) if base else spread * noise
        out[name] = jnp.asarray(drawn.astype(out[name].dtype))
    for name, factor in factors.items():
        out[name] = (out[name] * factor).astype(out[name].dtype)
    return out
```

```python
from contextlib import ExitStack

import concourse.bass as bass
from concourse import mybir

F32 = mybir.dt.float32
BF16 = mybir.dt.bfloat16
I32 = mybir.dt.int32
ALU = mybir.AluOpType
ACT = mybir.ActivationFunctionType

P = 128
B, NF, D, O = 512, 39, 16, 128
CTX, H1, H2 = 16, 512, 256
TILE = 128
TILES = B // TILE
ROTS = NF // 2 + 1
RPT = P // NF
KT = -(-ROTS // RPT)
KROWS = [NF * min(RPT, ROTS - RPT * k) for k in range(KT)]
R = NF * RPT
COLS = 512
GROUPS = TILE * D // COLS
GB = COLS // D
BB = P // D
SUB = GB // BB
MX = NF + 1
PRING = 3
PAR = 2
STEPS = TILES // PAR
SELS = KT + 1
Q = PAR * GROUPS
M1, M2 = H1 // P, H2 // P


def cin_tower(nc, A, out):
    ctx = ExitStack()
    with ctx:
        def sb(name, shape, dt=F32):
            return ctx.enter_context(nc.sbuf_tensor(name, shape, dt))

        def sem(name):
            return ctx.enter_context(nc.semaphore(name))

        ident = sb("ident", [P, P])
        ident16 = sb("ident16", [P, P], BF16)
        sel = sb("sel", [R, SELS, R], BF16)
        sel_m = sb("sel_m", [R, NF], BF16)
        own = sb("own", [P, BB])
        w0 = sb("w0", [R, KT, O])
        w0_mirror = sb("w0_mirror", [R, KT, O])
        w1 = sb("w1", [P, NF, O])
        wt1 = sb("wt1", [P, 2, H1])
        wt1_ctx = sb("wt1_ctx", [CTX, H1])
        wt2 = sb("wt2", [P, M1, H2])
        wt3 = sb("wt3", [P, M2])
        b1 = sb("b1", [P, M1])
        b2 = sb("b2", [P, M2])
        ctx_t = sb("ctx_t", [CTX, B])
        ids = sb("ids", [P, TILES, NF], I32)
        emb = sb("emb", [P, TILES, NF * D])
        rest = sb("rest", [P, D, NF])
        parts = sb("parts", [P, D, R], BF16)
        parts_t = [sb(f"parts_t{p}", [R, TILE, D], BF16) for p in range(PAR)]
        z_sb = [sb(f"z_sb{p}", [P, MX, TILE]) for p in range(PAR)]
        r2_sb = sb("r2_sb", [P, TILE])
        h1_sb = sb("h1_sb", [P, M1, TILE])
        h2_sb = sb("h2_sb", [P, M2, TILE])
        y_sb = sb("y_sb", [1, B])
        left = [sb(f"left{p}", [R, COLS]) for p in range(2)]
        pairs = [sb(f"pairs{p}", [R, COLS]) for p in range(PRING)]
        x1t_sb = sb("x1t_sb", [P, COLS])
        x1_sb = sb("x1_sb", [P, SUB, O])
        diag = [sb(f"diag{p}", [P, SUB, BB, MX]) for p in range(2)]

        bank = [ctx.enter_context(nc.psum_tensor(f"bank{n}", [P, 512], F32)) for n in range(8)]
        ps_t = bank[0][:, :].bitcast(BF16)
        ps_m = bank[0]
        ps_sel = [bank[1], bank[2]]
        ps_x = [bank[3], bank[4]]
        ps_mlp = bank[5]
        ps_z = [bank[6], bank[7]]

        s_ids = sem("s_ids")
        s_const = sem("s_const")
        s_w0 = sem("s_w0")
        s_w1 = sem("s_w1")
        s_wt = sem("s_wt")
        s_w0_sum = sem("s_w0_sum")
        s_ones = sem("s_ones")
        s_gather = [sem(f"s_gather{p}") for p in range(PAR)]
        s_hi = sem("s_hi")
        s_rest = sem("s_rest")
        s_mid = sem("s_mid")
        s_parts = sem("s_parts")
        s_pt = sem("s_pt")
        s_parts_t = sem("s_parts_t")
        s_sel = sem("s_sel")
        s_left = sem("s_left")
        s_pairs = sem("s_pairs")
        s_l1 = sem("s_l1")
        s_x1t = sem("s_x1t")
        s_xt = sem("s_xt")
        s_x1 = sem("s_x1")
        s_m = sem("s_m")
        s_diag = sem("s_diag")
        s_z = sem("s_z")
        s_z_sb = sem("s_z_sb")
        s_r2 = sem("s_r2")
        s_r2_sb = sem("s_r2_sb")
        s_h1 = sem("s_h1")
        s_h1_sb = sem("s_h1_sb")
        s_h2 = sem("s_h2")
        s_h2_sb = sem("s_h2_sb")
        s_y = sem("s_y")
        s_y_sb = sem("s_y_sb")
        s_out = sem("s_out")

        block = ctx.enter_context(nc.Block())

        @block.sync
        def _(sp):
            sp.dma_start(ids[:, :, :], A["ids"].rearrange("(t p) f -> p t f", p=P)).then_inc(s_ids, 16)
            sp.dma_start(ident16[:, :], A["ident16"].bitcast(BF16)).then_inc(s_const, 16)
            sp.dma_start(ident[:, :], A["ident"]).then_inc(s_const, 16)
            sp.dma_start(sel[:, :, :], A["sel"].bitcast(BF16)).then_inc(s_const, 16)
            sp.dma_start(sel_m[:, :], A["sel_m"].bitcast(BF16)).then_inc(s_const, 16)
            sp.dma_start(own[:, :], A["own"]).then_inc(s_const, 16)
            sp.dma_start(w0[:, :, :], A["w0"]).then_inc(s_w0, 16)
            sp.dma_start(w0_mirror[:, :, :], A["w0_mirror"]).then_inc(s_w0, 16)
            sp.dma_start(w1[:, :, :], A["w1"]).then_inc(s_w1, 16)
            sp.dma_start(wt1[:, :, :], A["wt1"]).then_inc(s_wt, 16)
            sp.dma_start(wt1_ctx[:, :], A["wt1_ctx"]).then_inc(s_wt, 16)
            sp.dma_start(wt2[:, :, :], A["wt2"]).then_inc(s_wt, 16)
            sp.dma_start(wt3[:, :], A["wt3"]).then_inc(s_wt, 16)
            sp.dma_start(b1[:, :], A["b1"]).then_inc(s_wt, 16)
            sp.dma_start(b2[:, :], A["b2"]).then_inc(s_wt, 16)
            sp.dma_start(ctx_t[:, :], A["ctx_t"]).then_inc(s_wt, 16)
            sp.wait_ge(s_y_sb, TILES)
            sp.dma_start(out.rearrange("b o -> o b"), y_sb[:, :]).then_inc(s_out, 16)
            sp.wait_ge(s_out, 16)

        @block.gpsimd
        def _(pool):
            pool.wait_ge(s_ids, 16)
            for t in range(TILES):
                if t >= PAR:
                    pool.wait_ge(s_gather[t % PAR], 16 * NF * (t // PAR))
                for f in range(NF):
                    nc.gpsimd.indirect_dma_start(
                        out=emb[:, t, f * D:(f + 1) * D], out_offset=None, in_=A[f"tbl_{f}"],
                        in_offset=bass.IndirectOffsetOnAxis(ap=ids[:, t, f:f + 1], axis=0),
                    ).then_inc(s_gather[t % PAR], 16)

        @block.scalar
        def _(act):
            def split_hi(i, p):
                act.wait_ge(s_gather[p], i * (16 * NF) + 16 * NF)
                if p:
                    act.wait_ge(s_pt, i * 4 + 2)
                nc.scalar.copy(parts[:, :, 0:NF], emb[:, i * PAR + p, :].rearrange("b (m d) -> b d m", d=D)).then_inc(s_hi, 1)

            def split_mid(i, p):
                act.wait_ge(s_rest, i * PAR + p + 1)
                nc.scalar.copy(parts[:, :, NF:2 * NF], rest[:, :, :]).then_inc(s_mid, 1)

            def take_left(i, q):
                act.wait_ge(s_sel, i * (Q * SELS) + q * SELS + 1)
                if q >= 2:
                    act.wait_ge(s_pairs, i * (Q * KT) + (q - 1) * KT)
                nc.scalar.copy(left[q % 2][:, :], ps_sel[(q * SELS) % 2][0:R, :]).then_inc(s_left, 1)

            def take_x1t(i, q):
                act.wait_ge(s_l1, i * (Q * KT) + (q + 1) * KT)
                nc.scalar.copy(x1t_sb[:, :], ps_x[q % 2][:, :]).then_inc(s_x1t, 1)

            def take_x1(i, q):
                act.wait_ge(s_xt, i * Q + q + 1)
                nc.scalar.copy(x1_sb[:, :, :], ps_x[q % 2][:, :].rearrange("p (j o) -> p j o", j=SUB)).then_inc(s_x1, 1)

            def take_z(i, q, j):
                n = q * SUB + j
                act.wait_ge(s_z, i * (Q * SUB) + n + 1)
                b0 = (q % GROUPS) * GB + j * BB
                nc.scalar.copy(z_sb[q // GROUPS][:, :, b0:b0 + BB].rearrange("n m b -> n b m"),
                               ps_z[n % 2][:, 0:BB * MX].rearrange("n (b m) -> n b m", m=MX)).then_inc(s_z_sb, 1)

            def take_r2(i, p):
                act.wait_ge(s_r2, i * PAR + p + 1)
                nc.scalar.copy(r2_sb[:, :], ps_mlp[:, 0:TILE]).then_inc(s_r2_sb, 1)

            def take_h1(i, p):
                act.wait_ge(s_h1, i * PAR + p + 1)
                for m in range(M1):
                    last = nc.scalar.activation(h1_sb[:, m, :], ps_mlp[:, m * TILE:(m + 1) * TILE], ACT.Relu,
                                                bias=b1[:, m:m + 1])
                last.then_inc(s_h1_sb, 1)

            def take_h2(i, p):
                act.wait_ge(s_h2, i * PAR + p + 1)
                for m in range(M2):
                    last = nc.scalar.activation(h2_sb[:, m, :], ps_mlp[:, m * TILE:(m + 1) * TILE], ACT.Relu,
                                                bias=b2[:, m:m + 1])
                last.then_inc(s_h2_sb, 1)

            def take_y(i, p):
                act.wait_ge(s_y, i * PAR + p + 1)
                nc.scalar.copy(y_sb[:, bass.ds(i * (PAR * TILE) + p * TILE, TILE)], ps_mlp[0:1, 0:TILE]).then_inc(s_y_sb, 1)

            act.wait_ge(s_wt, 16 * 7)
            with act.Fori(0, STEPS) as i:
                split_hi(i, 0)
                split_mid(i, 0)
                take_left(i, 0)
                for q in range(Q):
                    if q > 0:
                        take_x1t(i, q - 1)
                        take_x1(i, q - 1)
                        if q == GROUPS - 1:
                            split_hi(i, 1)
                            split_mid(i, 1)
                        if q == Q - 1:
                            take_h2(i, 0)
                        for j in range(SUB):
                            take_z(i, q - 1, j)
                    if q < Q - 1:
                        take_left(i, q + 1)
                    if q == GROUPS + 1:
                        take_r2(i, 0)
                    if q == GROUPS + 2:
                        take_h1(i, 0)
                    if q == Q - 1:
                        take_y(i, 0)
                take_x1t(i, Q - 1)
                take_x1(i, Q - 1)
                for j in range(SUB):
                    take_z(i, Q - 1, j)
                take_r2(i, 1)
                take_h1(i, 1)
                take_h2(i, 1)
                take_y(i, 1)

        @block.vector
        def _(dve):
            def split_rest(i, p):
                dve.wait_ge(s_hi, i * PAR + p + 1)
                nc.vector.tensor_tensor(rest[:, :, :], emb[:, i * PAR + p, :].rearrange("b (m d) -> b d m", d=D),
                                        parts[:, :, 0:NF], ALU.subtract).then_inc(s_rest, 1)

            def split_lo(i, p):
                dve.wait_ge(s_mid, i * PAR + p + 1)
                dve.wait_ge(s_rest, i * PAR + p + 1)
                nc.vector.tensor_tensor(parts[:, :, 2 * NF:3 * NF], rest[:, :, :], parts[:, :, NF:2 * NF],
                                        ALU.subtract).then_inc(s_parts, 1)

            def take_parts_t(i, p, half):
                dve.wait_ge(s_pt, i * 4 + p * 2 + half + 1)
                d0 = half * (D // 2)
                nc.vector.tensor_copy(parts_t[p][:, :, d0:d0 + D // 2].rearrange("r b d -> r d b"),
                                      ps_t[0:R, 0:D // 2 * TILE].rearrange("r (d b) -> r d b", b=TILE),
                                      ).then_inc(s_parts_t, 1)

            def multiply(i, q, k):
                n = q * KT + k
                dve.wait_ge(s_sel, i * (Q * SELS) + q * SELS + k + 2)
                if k == 0:
                    dve.wait_ge(s_left, i * Q + q + 1)
                if n >= PRING:
                    dve.wait_ge(s_l1, i * (Q * KT) + n - PRING + 1)
                r = KROWS[k]
                nc.vector.tensor_tensor(pairs[n % PRING][0:r, :], ps_sel[(q * SELS + k + 1) % 2][0:r, :],
                                        left[q % 2][0:r, :], ALU.mult).then_inc(s_pairs, 1)

            def spread(i, q):
                dve.wait_ge(s_m, i * Q + q + 1)
                if q >= 2:
                    dve.wait_ge(s_z, i * (Q * SUB) + (q - 1) * SUB)
                e_m = ps_m[:, 0:SUB * NF].rearrange("p (j m) -> p j m", m=NF).unsqueeze(2)
                nc.vector.tensor_tensor(diag[q % 2][:, :, :, 0:NF], e_m.to_broadcast([P, SUB, BB, NF]),
                                        own[:, :].unsqueeze(1).unsqueeze(3).to_broadcast([P, SUB, BB, NF]),
                                        ALU.mult).then_inc(s_diag, 1)

            dve.wait_ge(s_const, 16 * 5)
            for p in range(2):
                nc.vector.tensor_copy(diag[p][:, :, :, NF:MX],
                                      own[:, :].unsqueeze(1).unsqueeze(3).to_broadcast([P, SUB, BB, 1]),
                                      ).then_inc(s_ones, 1)
            dve.wait_ge(s_w0, 16 * 2)
            nc.vector.tensor_tensor(w0[:, :, :], w0[:, :, :], w0_mirror[:, :, :], ALU.add).then_inc(s_w0_sum, 1)
            with dve.Fori(0, STEPS) as i:
                split_rest(i, 0)
                split_lo(i, 0)
                take_parts_t(i, 0, 0)
                take_parts_t(i, 0, 1)
                for q in range(Q):
                    for k in range(KT):
                        multiply(i, q, k)
                        if q > 0 and k == 1:
                            spread(i, q - 1)
                        if q == GROUPS - 1 and k == 1:
                            split_rest(i, 1)
                        if q == GROUPS - 1 and k == 2:
                            split_lo(i, 1)
                        if q == GROUPS - 1 and k == 3:
                            take_parts_t(i, 1, 0)
                        if q == GROUPS - 1 and k == 4:
                            take_parts_t(i, 1, 1)
                spread(i, Q - 1)
                dve.wait_ge(s_z, i * (Q * SUB) + Q * SUB)

        @block.tensor
        def _(pe):
            def transpose_parts(i, p, half):
                n = p * 2 + half
                if half == 0:
                    pe.wait_ge(s_parts, i * PAR + p + 1)
                if n == 2:
                    pe.wait_ge(s_diag, i * Q + GROUPS - 1)
                elif n:
                    pe.wait_ge(s_parts_t, i * 4 + n)
                for d in range(D // 2):
                    last = nc.tensor.transpose(ps_t[0:R, d * TILE:(d + 1) * TILE],
                                               parts[:, half * (D // 2) + d, :], ident16[:, :])
                last.then_inc(s_pt, 1)

            def select(i, s):
                q, c = divmod(s, SELS)
                p, g = divmod(q, GROUPS)
                if c == 0 and g == 0:
                    pe.wait_ge(s_parts_t, i * 4 + p * 2 + 2)
                if s >= 2:
                    q2, c2 = divmod(s - 2, SELS)
                    if c2 == 0:
                        pe.wait_ge(s_left, i * Q + q2 + 1)
                    else:
                        pe.wait_ge(s_pairs, i * (Q * KT) + q2 * KT + c2)
                rows = KROWS[c - 1] if c else R
                nc.tensor.matmul(ps_sel[s % 2][0:rows, :], sel[:, c, 0:rows],
                                 parts_t[p][:, g * GB:(g + 1) * GB, :].rearrange("r b d -> r (b d)"),
                                 start=True, stop=True).then_inc(s_sel, 1)

            def layer1(i, q, k):
                n = q * KT + k
                if k == 0 and q >= 2:
                    pe.wait_ge(s_x1, i * Q + q - 1)
                pe.wait_ge(s_pairs, i * (Q * KT) + n + 1)
                nc.tensor.matmul(ps_x[q % 2][:, :], w0[0:KROWS[k], k, :], pairs[n % PRING][0:KROWS[k], :],
                                 start=(k == 0), stop=(k == KT - 1)).then_inc(s_l1, 1)

            def turn(i, q):
                p, g = divmod(q, GROUPS)
                pe.wait_ge(s_x1t, i * Q + q + 1)
                for j in range(SUB):
                    last = nc.tensor.transpose(ps_x[q % 2][:, j * O:(j + 1) * O], x1t_sb[:, j * P:(j + 1) * P],
                                               ident[:, :])
                last.then_inc(s_xt, 1)
                if g == 0:
                    pe.wait_ge(s_parts_t, i * 4 + p * 2 + 2)
                if q:
                    pe.wait_ge(s_diag, i * Q + q)
                for j in range(SUB):
                    b0 = g * GB + j * BB
                    last = nc.tensor.matmul(ps_m[:, j * NF:(j + 1) * NF],
                                            parts_t[p][:, b0:b0 + BB, :].rearrange("r b d -> r (b d)"), sel_m[:, :],
                                            start=True, stop=True)
                last.then_inc(s_m, 1)

            def interact(i, q, j):
                n = q * SUB + j
                if j == 0:
                    pe.wait_ge(s_x1, i * Q + q + 1)
                    pe.wait_ge(s_diag, i * Q + q + 1)
                if n >= 2:
                    pe.wait_ge(s_z_sb, i * (Q * SUB) + n - 1)
                nc.tensor.matmul(ps_z[n % 2][:, 0:BB * MX], x1_sb[:, j, :],
                                 diag[q % 2][:, j, :, :].rearrange("p b m -> p (b m)"),
                                 start=True, stop=True).then_inc(s_z, 1)

            def layer2(i, p, m0, m1):
                if m0 == 0:
                    pe.wait_ge(s_z_sb, (i * PAR + p + 1) * (GROUPS * SUB))
                for m in range(m0, m1):
                    last = nc.tensor.matmul(ps_mlp[:, 0:TILE], w1[:, m, :], z_sb[p][:, m, :],
                                            start=(m == 0), stop=(m == NF - 1))
                if m1 == NF:
                    last.then_inc(s_r2, 1)

            def hidden1(i, p):
                pe.wait_ge(s_r2_sb, i * PAR + p + 1)
                for m in range(M1):
                    o, w = ps_mlp[:, m * TILE:(m + 1) * TILE], slice(m * P, (m + 1) * P)
                    nc.tensor.matmul(o, wt1[:, 0, w], z_sb[p][:, NF, :], start=True, stop=False)
                    nc.tensor.matmul(o, wt1[:, 1, w], r2_sb[:, :], start=False, stop=False)
                    last = nc.tensor.matmul(o, wt1_ctx[:, w], ctx_t[:, bass.ds(i * (PAR * TILE) + p * TILE, TILE)],
                                            start=False, stop=True)
                last.then_inc(s_h1, 1)

            def hidden2(i, p):
                pe.wait_ge(s_h1_sb, i * PAR + p + 1)
                for m in range(M2):
                    for c in range(M1):
                        last = nc.tensor.matmul(ps_mlp[:, m * TILE:(m + 1) * TILE], wt2[:, c, m * P:(m + 1) * P],
                                                h1_sb[:, c, :], start=(c == 0), stop=(c == M1 - 1))
                last.then_inc(s_h2, 1)

            def output(i, p):
                pe.wait_ge(s_h2_sb, i * PAR + p + 1)
                for c in range(M2):
                    last = nc.tensor.matmul(ps_mlp[0:1, 0:TILE], wt3[:, c:c + 1], h2_sb[:, c, :],
                                            start=(c == 0), stop=(c == M2 - 1))
                last.then_inc(s_y, 1)

            pe.wait_ge(s_const, 16 * 5)
            pe.wait_ge(s_w0_sum, 1)
            pe.wait_ge(s_ones, 2)
            pe.wait_ge(s_w1, 16)
            pe.wait_ge(s_wt, 16 * 7)
            with pe.Fori(0, STEPS) as i:
                transpose_parts(i, 0, 0)
                transpose_parts(i, 0, 1)
                for s in range(3):
                    select(i, s)
                for q in range(Q):
                    for k in range(KT):
                        if q == GROUPS - 1 and k == 3:
                            transpose_parts(i, 1, 0)
                        if q == GROUPS - 1 and k == 4:
                            transpose_parts(i, 1, 1)
                        if q and k == 0:
                            select(i, q * SELS + 2)
                        if q * SELS + k + 3 < Q * SELS:
                            select(i, q * SELS + k + 3)
                        layer1(i, q, k)
                        if q > 0 and k == 1:
                            turn(i, q - 1)
                        if q > 0 and 3 <= k < 3 + SUB:
                            interact(i, q - 1, k - 3)
                        if q == GROUPS + 1 and k < 5:
                            layer2(i, 0, 8 * k, min(8 * k + 8, NF))
                        if q == GROUPS + 2 and k == 2:
                            hidden1(i, 0)
                        if q == Q - 1 and k == 2:
                            hidden2(i, 0)
                        if q == Q - 1 and k == 6:
                            output(i, 0)
                turn(i, Q - 1)
                for j in range(SUB):
                    interact(i, Q - 1, j)
                layer2(i, 1, 0, NF)
                hidden1(i, 1)
                hidden2(i, 1)
                output(i, 1)


_TABLES = [f"tbl_{f}" for f in range(NF)]


def _laid_out(inputs):
    import numpy as np

    a = {name: np.ascontiguousarray(inputs[name]) for name in ["ids"] + _TABLES}
    c = {}
    w = np.asarray(inputs["L0_rec_W0"])
    w0 = np.zeros((KT * R, O), w.dtype)
    w0_mirror = np.zeros((KT * R, O), w.dtype)
    k, m = np.divmod(np.arange(ROTS * NF), NF)
    n = (m + k) % NF
    w0[:ROTS * NF] = w[m * NF + n]
    w0_mirror[NF:ROTS * NF] = w[(n * NF + m)[NF:]]
    a["w0"] = np.ascontiguousarray(w0.reshape(KT, R, O).transpose(1, 0, 2))
    a["w0_mirror"] = np.ascontiguousarray(w0_mirror.reshape(KT, R, O).transpose(1, 0, 2))
    a["w1"] = np.ascontiguousarray(np.asarray(inputs["L0_rec_W1"]).reshape(NF, O, O).transpose(1, 0, 2))
    wt1 = np.asarray(inputs["W_top1"])
    a["wt1"] = np.ascontiguousarray(wt1[:2 * O].reshape(2, P, H1).transpose(1, 0, 2))
    a["wt1_ctx"] = np.ascontiguousarray(wt1[2 * O:])
    a["wt2"] = np.ascontiguousarray(np.asarray(inputs["W_top2"]).reshape(M1, P, H2).transpose(1, 0, 2))
    a["wt3"] = np.ascontiguousarray(np.asarray(inputs["W_top3"]).reshape(M2, P).T)
    a["b1"] = np.ascontiguousarray(np.asarray(inputs["b_top1"]).reshape(M1, P).T)
    a["b2"] = np.ascontiguousarray(np.asarray(inputs["b_top2"]).reshape(M2, P).T)
    a["ctx_t"] = np.ascontiguousarray(np.asarray(inputs["dense_ctx"]).T)
    one = 0x3F80
    sel = np.zeros((R, SELS, R), np.uint16)
    for col in range(R):
        r, m = divmod(col, NF)
        for part in range(3):
            sel[part * NF + m, 0, col] = one
            for t in range(KT):
                sel[part * NF + (m + RPT * t + r) % NF, 1 + t, col] = one
    c["sel"] = sel
    sel_m = np.zeros((R, NF), np.uint16)
    for row in range(R):
        sel_m[row, row % NF] = one
    c["sel_m"] = sel_m
    own = np.zeros((P, BB), np.float32)
    own[np.arange(P), np.arange(P) // D] = 1
    c["own"] = own
    c["ident"] = np.eye(P, dtype=np.float32)
    c["ident16"] = np.eye(P, dtype=np.uint16) * one
    a.update(c)
    return a


def kernel(**inputs):
    import concourse.bacc as _bacc
    from concourse.bass_utils import run_bass_kernel_spmd as _run

    nc = _bacc.Bacc("TRN2", target_bir_lowering=False, num_devices=1)
    arrays, args = {}, {}
    for name, a in _laid_out(inputs).items():
        arrays[f"in_{name}"] = a
        args[name] = nc.dram_tensor(f"in_{name}", a.shape, mybir.dt.from_np(a.dtype), kind="ExternalInput").ap()
    y = nc.dram_tensor("out_y", (B, 1), F32, kind="ExternalOutput").ap()
    cin_tower(nc, args, y)
    return _run(nc, [arrays], core_ids=[0]).results[0]["out_y"]
```

```python
from contextlib import ExitStack

import concourse.bass as bass
from concourse import mybir

F32 = mybir.dt.float32
F32R = mybir.dt.float32r
BF16 = mybir.dt.bfloat16
I32 = mybir.dt.int32
ALU = mybir.AluOpType
ACT = mybir.ActivationFunctionType

P = 128
B, NF, D, O = 512, 39, 16, 128
CTX, H1, H2 = 16, 512, 256
TILE = 128
TILES = B // TILE
ROTS = NF // 2 + 1
RPT = P // NF
KT = -(-ROTS // RPT)
KROWS = [NF * min(RPT, ROTS - RPT * k) for k in range(KT)]
R = NF * RPT
COLS = 512
GROUPS = TILE * D // COLS
GB = COLS // D
BB = P // D
SUB = GB // BB
MX = NF + 1
PRING = 4
AHEAD = 3
SELS = KT + 1
GS = TILES * GROUPS
M1, M2 = H1 // P, H2 // P


def posted(q):
    return q - 1 if q and q != GROUPS else None


def early(q):
    return q % GROUPS == GROUPS - 1 and GROUPS < q < GS - 1


def turns():
    out = [("parts", 0, 0), ("parts", 0, 1)]
    for q in range(GS):
        if posted(q) is not None:
            out.append(("e", q - 1, 0))
        if early(q):
            out += [("parts", (q + 1) // GROUPS, half) for half in range(2)]
        if posted(q) is not None:
            out += [("z", q - 1, j) for j in range(SUB)]
        if q == GROUPS - 1 or q == GS - 1:
            out += [("e", q, 0)] + [("z", q, j) for j in range(SUB)]
        if q == GROUPS - 1:
            out += [("parts", 1, 0), ("parts", 1, 1)]
    return out


def ahead(q):
    return GROUPS if q < GROUPS else GS


def cin_tower(nc, A, out):
    ctx = ExitStack()
    with ctx:
        def sb(name, shape, dt=F32):
            return ctx.enter_context(nc.sbuf_tensor(name, shape, dt))

        def sem(name):
            return ctx.enter_context(nc.semaphore(name))

        ident = sb("ident", [P, P])
        ident16 = sb("ident16", [P, P], BF16)
        sel = sb("sel", [R, SELS, R], BF16)
        sel_m = sb("sel_m", [R, NF], BF16)
        own = sb("own", [P, BB])
        w0 = sb("w0", [R, KT, O])
        w0_hi = sb("w0_hi", [R, KT, O], F32R)
        w0_lo = sb("w0_lo", [R, KT, O], F32R)
        w0_mirror = sb("w0_mirror", [R, KT, O])
        w1 = sb("w1", [P, NF, O])
        wt1 = sb("wt1", [P, 2, H1])
        wt1_ctx = sb("wt1_ctx", [CTX, H1])
        wt2 = sb("wt2", [P, M1, H2])
        wt3 = sb("wt3", [P, M2])
        b1 = sb("b1", [P, M1])
        b2 = sb("b2", [P, M2])
        ctx_t = sb("ctx_t", [CTX, B])
        ids = sb("ids", [P, TILES, NF], I32)
        emb = sb("emb", [P, TILES, NF * D])
        rest = sb("rest", [P, D, NF])
        parts = sb("parts", [P, D, R], BF16)
        parts_t = [sb(f"parts_t{p}", [R, TILE, D], BF16) for p in range(2)]
        z_sb = [sb(f"z_sb{p}", [P, MX, TILE]) for p in range(2)]
        r2_sb = sb("r2_sb", [P, TILE])
        h1_sb = sb("h1_sb", [P, M1, TILE])
        h2_sb = sb("h2_sb", [P, M2, TILE])
        y_sb = sb("y_sb", [1, B])
        left = [sb(f"left{p}", [R, COLS]) for p in range(2)]
        pairs = [sb(f"pairs{p}", [R, COLS]) for p in range(PRING)]
        pairs_hi = [sb(f"pairs_hi{p}", [R, COLS], F32R) for p in range(PRING)]
        pairs_lo = [sb(f"pairs_lo{p}", [R, COLS], F32R) for p in range(PRING)]
        x1t_sb = sb("x1t_sb", [P, COLS])
        x1_sb = sb("x1_sb", [P, SUB, O])
        diag = [sb(f"diag{p}", [P, SUB, BB, MX]) for p in range(2)]

        bank = [ctx.enter_context(nc.psum_tensor(f"bank{n}", [P, 512], F32)) for n in range(8)]
        ps_sel = bank[0:AHEAD]
        ps_x = bank[3:5]
        ps_mlp = bank[5]
        ps_turn = bank[6:8]
        turn_order = turns()

        def turn_bank(*entry):
            return ps_turn[turn_order.index(entry) % 2]

        s_ids = sem("s_ids")
        s_const = sem("s_const")
        s_w0 = sem("s_w0")
        s_w1 = sem("s_w1")
        s_wt = sem("s_wt")
        s_w0_sum = sem("s_w0_sum")
        s_w0_hi = sem("s_w0_hi")
        s_w0_parts = sem("s_w0_parts")
        s_ones = sem("s_ones")
        s_gather = [sem(f"s_gather{t}") for t in range(TILES)]
        s_hi = sem("s_hi")
        s_rest = sem("s_rest")
        s_mid = sem("s_mid")
        s_parts = sem("s_parts")
        s_pt = sem("s_pt")
        s_parts_t0 = sem("s_parts_t0")
        s_parts_t1 = sem("s_parts_t1")
        s_sel = sem("s_sel")
        s_left = sem("s_left")
        s_pairs = sem("s_pairs")
        s_pairs_hi = sem("s_pairs_hi")
        s_pairs_lo = sem("s_pairs_lo")
        s_l1 = sem("s_l1")
        s_x1t = sem("s_x1t")
        s_xt = sem("s_xt")
        s_x1 = sem("s_x1")
        s_m = sem("s_m")
        s_diag = sem("s_diag")
        s_z = sem("s_z")
        s_z_sb = sem("s_z_sb")
        s_r2 = sem("s_r2")
        s_r2_sb = sem("s_r2_sb")
        s_h1 = sem("s_h1")
        s_h1_sb = sem("s_h1_sb")
        s_h2 = sem("s_h2")
        s_h2_sb = sem("s_h2_sb")
        s_y = sem("s_y")
        s_y_sb = sem("s_y_sb")
        s_out = sem("s_out")

        block = ctx.enter_context(nc.Block())

        @block.sync
        def _(sp):
            sp.dma_start(ids[:, :, :], A["ids"].rearrange("(t p) f -> p t f", p=P)).then_inc(s_ids, 16)
            sp.dma_start(ident16[:, :], A["ident16"].bitcast(BF16)).then_inc(s_const, 16)
            sp.dma_start(ident[:, :], A["ident"]).then_inc(s_const, 16)
            sp.dma_start(sel[:, :, :], A["sel"].bitcast(BF16)).then_inc(s_const, 16)
            sp.dma_start(sel_m[:, :], A["sel_m"].bitcast(BF16)).then_inc(s_const, 16)
            sp.dma_start(own[:, :], A["own"]).then_inc(s_const, 16)
            sp.dma_start(w0[:, :, :], A["w0"]).then_inc(s_w0, 16)
            sp.dma_start(w0_mirror[:, :, :], A["w0_mirror"]).then_inc(s_w0, 16)
            sp.dma_start(w1[:, :, :], A["w1"]).then_inc(s_w1, 16)
            sp.dma_start(wt1[:, :, :], A["wt1"]).then_inc(s_wt, 16)
            sp.dma_start(wt1_ctx[:, :], A["wt1_ctx"]).then_inc(s_wt, 16)
            sp.dma_start(wt2[:, :, :], A["wt2"]).then_inc(s_wt, 16)
            sp.dma_start(wt3[:, :], A["wt3"]).then_inc(s_wt, 16)
            sp.dma_start(b1[:, :], A["b1"]).then_inc(s_wt, 16)
            sp.dma_start(b2[:, :], A["b2"]).then_inc(s_wt, 16)
            sp.dma_start(ctx_t[:, :], A["ctx_t"]).then_inc(s_wt, 16)
            sp.wait_ge(s_y_sb, TILES)
            sp.dma_start(out.rearrange("b o -> o b"), y_sb[:, :]).then_inc(s_out, 16)
            sp.wait_ge(s_out, 16)

        @block.gpsimd
        def _(pool):
            pool.wait_ge(s_ids, 16)
            for t in range(TILES):
                for f in range(NF):
                    nc.gpsimd.indirect_dma_start(
                        out=emb[:, t, f * D:(f + 1) * D], out_offset=None, in_=A[f"tbl_{f}"],
                        in_offset=bass.IndirectOffsetOnAxis(ap=ids[:, t, f:f + 1], axis=0),
                    ).then_inc(s_gather[t], 16)

        @block.scalar
        def _(act):
            def split_hi(t):
                act.wait_ge(s_gather[t], 16 * NF)
                if t:
                    act.wait_ge(s_pt, 2 * t)
                nc.scalar.copy(parts[:, :, 0:NF], emb[:, t, :].rearrange("b (m d) -> b d m", d=D)).then_inc(s_hi, 1)

            def split_mid(t):
                act.wait_ge(s_rest, t + 1)
                nc.scalar.copy(parts[:, :, NF:2 * NF], rest[:, :, :]).then_inc(s_mid, 1)

            def take_parts_t1(t):
                act.wait_ge(s_pt, 2 * t + 2)
                ps = turn_bank("parts", t, 1)[0:R, :].bitcast(BF16)
                nc.scalar.copy(parts_t[t % 2][:, :, D // 2:D].rearrange("r b d -> r d b"),
                               ps.rearrange("r (d b) -> r d b", b=TILE)).then_inc(s_parts_t1, 1)

            def take_left(q):
                act.wait_ge(s_sel, q * SELS + 1)
                if q >= 2:
                    act.wait_ge(s_pairs, (q - 1) * KT)
                nc.scalar.copy(left[q % 2][:, :], ps_sel[q * SELS % AHEAD][0:R, :]).then_inc(s_left, 1)

            def pair_hi(n):
                r = KROWS[n % KT]
                act.wait_ge(s_pairs, n + 1)
                if n >= PRING:
                    act.wait_ge(s_l1, n - PRING + 1)
                nc.scalar.copy(pairs_hi[n % PRING][0:r, :], pairs[n % PRING][0:r, :]).then_inc(s_pairs_hi, 1)

            def take_x1t(q):
                act.wait_ge(s_l1, (q + 1) * KT)
                nc.scalar.copy(x1t_sb[:, :], ps_x[q % 2][:, :]).then_inc(s_x1t, 1)

            def take_x1(q):
                act.wait_ge(s_xt, q + 1)
                nc.scalar.copy(x1_sb[:, :, :], ps_x[q % 2][:, :].rearrange("p (j o) -> p j o", j=SUB)).then_inc(s_x1, 1)

            def take_z(q, j):
                act.wait_ge(s_z, q * SUB + j + 1)
                t, g = divmod(q, GROUPS)
                b0 = g * GB + j * BB
                nc.scalar.copy(z_sb[t % 2][:, :, b0:b0 + BB].rearrange("n m b -> n b m"),
                               turn_bank("z", q, j)[:, 0:BB * MX].rearrange("n (b m) -> n b m", m=MX)).then_inc(s_z_sb, 1)

            def take_r2(t):
                act.wait_ge(s_r2, t + 1)
                nc.scalar.copy(r2_sb[:, :], ps_mlp[:, 0:TILE]).then_inc(s_r2_sb, 1)

            def take_h1(t):
                act.wait_ge(s_h1, t + 1)
                for m in range(M1):
                    last = nc.scalar.activation(h1_sb[:, m, :], ps_mlp[:, m * TILE:(m + 1) * TILE], ACT.Relu,
                                                bias=b1[:, m:m + 1])
                last.then_inc(s_h1_sb, 1)

            def take_h2(t):
                act.wait_ge(s_h2, t + 1)
                for m in range(M2):
                    last = nc.scalar.activation(h2_sb[:, m, :], ps_mlp[:, m * TILE:(m + 1) * TILE], ACT.Relu,
                                                bias=b2[:, m:m + 1])
                last.then_inc(s_h2_sb, 1)

            def take_y(t):
                act.wait_ge(s_y, t + 1)
                nc.scalar.copy(y_sb[:, t * TILE:(t + 1) * TILE], ps_mlp[0:1, 0:TILE]).then_inc(s_y_sb, 1)

            act.wait_ge(s_wt, 16 * 7)
            split_hi(0)
            split_mid(0)
            take_parts_t1(0)
            take_left(0)
            hi = 0
            for q in range(GS):
                for k in range(KT):
                    while hi < min(q * KT + k + AHEAD, ahead(q) * KT):
                        pair_hi(hi)
                        hi += 1
                    if k == AHEAD and not early(q) and q + 1 < ahead(q):
                        take_left(q + 1)
                    if posted(q) is not None:
                        if k == 0:
                            take_x1t(q - 1)
                        if k == 1:
                            take_x1(q - 1)
                        if k >= KT - SUB:
                            take_z(q - 1, k - (KT - SUB))
                    if early(q):
                        t = (q + 1) // GROUPS
                        if k == 0:
                            split_hi(t)
                        if k == 1:
                            split_mid(t)
                        if k == 3:
                            take_parts_t1(t)
                        if k == 4:
                            take_left(q + 1)
                    if q == GROUPS and k == 1:
                        take_h1(0)
                    if q == GROUPS and k == 4:
                        take_h2(0)
                    if q == GROUPS + 1 and k == 0:
                        take_y(0)
                    t, g = q // GROUPS - 1, q % GROUPS
                    if t >= 1:
                        if g == 2 and k == 6:
                            take_r2(t)
                        if g == 3 and k == 1:
                            take_h1(t)
                        if g == 3 and k == 4:
                            take_h2(t)
                        if g == 3 and k == 6:
                            take_y(t)
                if q in (GROUPS - 1, GS - 1):
                    take_x1t(q)
                    take_x1(q)
                    for j in range(SUB):
                        take_z(q, j)
                if q == GROUPS - 1:
                    split_hi(1)
                    split_mid(1)
                    take_r2(0)
                    take_parts_t1(1)
                    take_left(q + 1)
            take_r2(TILES - 1)
            take_h1(TILES - 1)
            take_h2(TILES - 1)
            take_y(TILES - 1)

        @block.vector
        def _(dve):
            def split_rest(t):
                dve.wait_ge(s_hi, t + 1)
                nc.vector.tensor_tensor(rest[:, :, :], emb[:, t, :].rearrange("b (m d) -> b d m", d=D),
                                        parts[:, :, 0:NF], ALU.subtract).then_inc(s_rest, 1)

            def split_lo(t):
                dve.wait_ge(s_mid, t + 1)
                dve.wait_ge(s_rest, t + 1)
                nc.vector.tensor_tensor(parts[:, :, 2 * NF:3 * NF], rest[:, :, :], parts[:, :, NF:2 * NF],
                                        ALU.subtract).then_inc(s_parts, 1)

            def take_parts_t0(t):
                dve.wait_ge(s_pt, 2 * t + 1)
                ps = turn_bank("parts", t, 0)[0:R, :].bitcast(BF16)
                nc.vector.tensor_copy(parts_t[t % 2][:, :, 0:D // 2].rearrange("r b d -> r d b"),
                                      ps.rearrange("r (d b) -> r d b", b=TILE)).then_inc(s_parts_t0, 1)

            def multiply(n):
                q, k = divmod(n, KT)
                r, s = KROWS[k], q * SELS + k + 1
                dve.wait_ge(s_sel, s + 1)
                if k == 0:
                    dve.wait_ge(s_left, q + 1)
                if n >= PRING:
                    dve.wait_ge(s_pairs_hi, n - PRING + 1)
                    dve.wait_ge(s_pairs_lo, n - PRING + 1)
                nc.vector.tensor_tensor(pairs[n % PRING][0:r, :], ps_sel[s % AHEAD][0:r, :],
                                        left[q % 2][0:r, :], ALU.mult).then_inc(s_pairs, 1)

            def pair_lo(n):
                r = KROWS[n % KT]
                dve.wait_ge(s_pairs_hi, n + 1)
                dve.wait_ge(s_pairs, n + 1)
                if n >= PRING:
                    dve.wait_ge(s_l1, n - PRING + 1)
                nc.vector.tensor_tensor(pairs_lo[n % PRING][0:r, :], pairs[n % PRING][0:r, :],
                                        pairs_hi[n % PRING][0:r, :].bitcast(F32), ALU.subtract).then_inc(s_pairs_lo, 1)

            def spread(q, j):
                if j == 0:
                    dve.wait_ge(s_m, q + 1)
                if q >= 2:
                    dve.wait_ge(s_z, (q - 2) * SUB + j + 1)
                e_m = turn_bank("e", q, 0)[:, j * NF:(j + 1) * NF].unsqueeze(1)
                nc.vector.tensor_tensor(diag[q % 2][:, j, :, 0:NF], e_m.to_broadcast([P, BB, NF]),
                                        own[:, :].unsqueeze(2).to_broadcast([P, BB, NF]),
                                        ALU.mult).then_inc(s_diag, 1)

            dve.wait_ge(s_const, 16 * 5)
            for p in range(2):
                nc.vector.tensor_copy(diag[p][:, :, :, NF:MX],
                                      own[:, :].unsqueeze(1).unsqueeze(3).to_broadcast([P, SUB, BB, 1]),
                                      ).then_inc(s_ones, 1)
            dve.wait_ge(s_w0, 16 * 2)
            nc.vector.tensor_tensor(w0[:, :, :], w0[:, :, :], w0_mirror[:, :, :], ALU.add).then_inc(s_w0_sum, 1)
            dve.wait_ge(s_w0_sum, 1)
            nc.vector.tensor_copy(w0_hi[:, :, :], w0[:, :, :]).then_inc(s_w0_hi, 1)
            dve.wait_ge(s_w0_hi, 1)
            nc.vector.tensor_tensor(w0_lo[:, :, :], w0[:, :, :], w0_hi[:, :, :].bitcast(F32),
                                    ALU.subtract).then_inc(s_w0_parts, 1)
            split_rest(0)
            split_lo(0)
            take_parts_t0(0)
            made = low = 0
            for q in range(GS):
                for k in range(KT):
                    while made < min(q * KT + k + AHEAD + 1, ahead(q) * KT):
                        multiply(made)
                        made += 1
                        if low < made - 1:
                            pair_lo(low)
                            low += 1
                    if made == ahead(q) * KT and low < made:
                        pair_lo(low)
                        low += 1
                    if posted(q) is not None and k < 2:
                        for j in range(SUB // 2):
                            spread(q - 1, k * (SUB // 2) + j)
                    if early(q):
                        t = (q + 1) // GROUPS
                        if k == 0:
                            split_rest(t)
                        if k == 1:
                            split_lo(t)
                        if k == 2:
                            take_parts_t0(t)
                if q in (GROUPS - 1, GS - 1):
                    for j in range(SUB):
                        spread(q, j)
                if q == GROUPS - 1:
                    split_rest(1)
                    split_lo(1)
                    take_parts_t0(1)

        @block.tensor
        def _(pe):
            def take_turn(*entry):
                e = turn_order.index(entry)
                if e >= 2:
                    kind, n, j = turn_order[e - 2]
                    if kind == "parts":
                        pe.wait_ge(s_parts_t1 if j else s_parts_t0, n + 1)
                    elif kind == "e":
                        pe.wait_ge(s_diag, (n + 1) * SUB)
                    else:
                        pe.wait_ge(s_z_sb, n * SUB + j + 1)
                return ps_turn[e % 2]

            def transpose_parts(t, half):
                if half == 0:
                    pe.wait_ge(s_parts, t + 1)
                ps = take_turn("parts", t, half)[0:R, :].bitcast(BF16)
                for d in range(D // 2):
                    last = nc.tensor.transpose(ps[:, d * TILE:(d + 1) * TILE],
                                               parts[:, half * (D // 2) + d, :], ident16[:, :])
                last.then_inc(s_pt, 1)

            def select(s):
                q, c = divmod(s, SELS)
                t, g = divmod(q, GROUPS)
                if c == 0 and g == 0:
                    pe.wait_ge(s_parts_t0, t + 1)
                    pe.wait_ge(s_parts_t1, t + 1)
                if s >= AHEAD:
                    q2, c2 = divmod(s - AHEAD, SELS)
                    if c2 == 0:
                        pe.wait_ge(s_left, q2 + 1)
                    else:
                        pe.wait_ge(s_pairs, q2 * KT + c2)
                rows = KROWS[c - 1] if c else R
                nc.tensor.matmul(ps_sel[s % AHEAD][0:rows, :], sel[:, c, 0:rows],
                                 parts_t[t % 2][:, g * GB:(g + 1) * GB, :].rearrange("r b d -> r (b d)"),
                                 start=True, stop=True).then_inc(s_sel, 1)

            def layer1(q, k):
                n, r = q * KT + k, KROWS[k]
                if k == 0 and q >= 2:
                    pe.wait_ge(s_x1, q - 1)
                hi, lo = pairs_hi[n % PRING][0:r, :], pairs_lo[n % PRING][0:r, :]
                pe.wait_ge(s_pairs_hi, n + 1)
                nc.tensor.matmul(ps_x[q % 2][:, :], w0_lo[0:r, k, :], hi, start=(k == 0), stop=False)
                nc.tensor.matmul(ps_x[q % 2][:, :], w0_hi[0:r, k, :], hi, start=False, stop=False)
                pe.wait_ge(s_pairs_lo, n + 1)
                nc.tensor.matmul(ps_x[q % 2][:, :], w0_hi[0:r, k, :], lo, start=False,
                                 stop=(k == KT - 1)).then_inc(s_l1, 1)

            def turn_x1(q):
                pe.wait_ge(s_x1t, q + 1)
                for j in range(SUB):
                    last = nc.tensor.transpose(ps_x[q % 2][:, j * O:(j + 1) * O], x1t_sb[:, j * P:(j + 1) * P],
                                               ident[:, :])
                last.then_inc(s_xt, 1)

            def turn_e(q):
                t, g = divmod(q, GROUPS)
                ps = take_turn("e", q, 0)
                for j in range(SUB):
                    b0 = g * GB + j * BB
                    last = nc.tensor.matmul(ps[:, j * NF:(j + 1) * NF],
                                            parts_t[t % 2][:, b0:b0 + BB, :].rearrange("r b d -> r (b d)"), sel_m[:, :],
                                            start=True, stop=True)
                last.then_inc(s_m, 1)

            def interact(q, j):
                if j == 0:
                    pe.wait_ge(s_x1, q + 1)
                pe.wait_ge(s_diag, q * SUB + j + 1)
                nc.tensor.matmul(take_turn("z", q, j)[:, 0:BB * MX], x1_sb[:, j, :],
                                 diag[q % 2][:, j, :, :].rearrange("p b m -> p (b m)"),
                                 start=True, stop=True).then_inc(s_z, 1)

            def layer2(t, m0, m1):
                if m0 == 0:
                    pe.wait_ge(s_z_sb, (t + 1) * (GROUPS * SUB))
                    if t:
                        pe.wait_ge(s_y_sb, t)
                for m in range(m0, m1):
                    last = nc.tensor.matmul(ps_mlp[:, 0:TILE], w1[:, m, :], z_sb[t % 2][:, m, :],
                                            start=(m == 0), stop=(m == NF - 1))
                if m1 == NF:
                    last.then_inc(s_r2, 1)

            def hidden1(t):
                pe.wait_ge(s_r2_sb, t + 1)
                for m in range(M1):
                    o, w = ps_mlp[:, m * TILE:(m + 1) * TILE], slice(m * P, (m + 1) * P)
                    nc.tensor.matmul(o, wt1[:, 0, w], z_sb[t % 2][:, NF, :], start=True, stop=False)
                    nc.tensor.matmul(o, wt1[:, 1, w], r2_sb[:, :], start=False, stop=False)
                    last = nc.tensor.matmul(o, wt1_ctx[:, w], ctx_t[:, t * TILE:(t + 1) * TILE],
                                            start=False, stop=True)
                last.then_inc(s_h1, 1)

            def hidden2(t):
                pe.wait_ge(s_h1_sb, t + 1)
                for m in range(M2):
                    for c in range(M1):
                        last = nc.tensor.matmul(ps_mlp[:, m * TILE:(m + 1) * TILE], wt2[:, c, m * P:(m + 1) * P],
                                                h1_sb[:, c, :], start=(c == 0), stop=(c == M1 - 1))
                last.then_inc(s_h2, 1)

            def output(t):
                pe.wait_ge(s_h2_sb, t + 1)
                for c in range(M2):
                    last = nc.tensor.matmul(ps_mlp[0:1, 0:TILE], wt3[:, c:c + 1], h2_sb[:, c, :],
                                            start=(c == 0), stop=(c == M2 - 1))
                last.then_inc(s_y, 1)

            pe.wait_ge(s_const, 16 * 5)
            pe.wait_ge(s_w0_parts, 1)
            pe.wait_ge(s_ones, 2)
            pe.wait_ge(s_w1, 16)
            pe.wait_ge(s_wt, 16 * 7)
            transpose_parts(0, 0)
            transpose_parts(0, 1)
            picked = 0
            for q in range(GS):
                if posted(q) is not None:
                    turn_e(q - 1)
                for k in range(KT):
                    while picked < min(q * SELS + k + 2 + AHEAD + (k >= AHEAD + early(q)), ahead(q) * SELS):
                        select(picked)
                        picked += 1
                    layer1(q, k)
                    if early(q) and 2 <= k <= 3:
                        transpose_parts((q + 1) // GROUPS, k - 2)
                    if posted(q) is not None:
                        if k == 1:
                            turn_x1(q - 1)
                        if k >= KT - SUB:
                            interact(q - 1, k - (KT - SUB))
                    if q == GROUPS and k == 3:
                        hidden2(0)
                    if q == GROUPS and k == 6:
                        output(0)
                    t, g = q // GROUPS - 1, q % GROUPS
                    if t >= 1:
                        if g in (1, 2):
                            m = ((g - 1) * KT + k) * 3
                            if m < NF:
                                layer2(t, m, min(m + 3, NF))
                        if g == 3 and k == 0:
                            hidden1(t)
                        if g == 3 and k == 3:
                            hidden2(t)
                        if g == 3 and k == 5:
                            output(t)
                if q in (GROUPS - 1, GS - 1):
                    turn_e(q)
                    turn_x1(q)
                    for j in range(SUB):
                        interact(q, j)
                    layer2(q // GROUPS, 0, NF)
                if q == GROUPS - 1:
                    transpose_parts(1, 0)
                    transpose_parts(1, 1)
                    hidden1(0)
            hidden1(TILES - 1)
            hidden2(TILES - 1)
            output(TILES - 1)


_TABLES = [f"tbl_{f}" for f in range(NF)]


def _laid_out(inputs):
    import numpy as np

    a = {name: np.ascontiguousarray(inputs[name]) for name in ["ids"] + _TABLES}
    c = {}
    w = np.asarray(inputs["L0_rec_W0"])
    w0 = np.zeros((KT * R, O), w.dtype)
    w0_mirror = np.zeros((KT * R, O), w.dtype)
    k, m = np.divmod(np.arange(ROTS * NF), NF)
    n = (m + k) % NF
    w0[:ROTS * NF] = w[m * NF + n]
    w0_mirror[NF:ROTS * NF] = w[(n * NF + m)[NF:]]
    a["w0"] = np.ascontiguousarray(w0.reshape(KT, R, O).transpose(1, 0, 2))
    a["w0_mirror"] = np.ascontiguousarray(w0_mirror.reshape(KT, R, O).transpose(1, 0, 2))
    a["w1"] = np.ascontiguousarray(np.asarray(inputs["L0_rec_W1"]).reshape(NF, O, O).transpose(1, 0, 2))
    wt1 = np.asarray(inputs["W_top1"])
    a["wt1"] = np.ascontiguousarray(wt1[:2 * O].reshape(2, P, H1).transpose(1, 0, 2))
    a["wt1_ctx"] = np.ascontiguousarray(wt1[2 * O:])
    a["wt2"] = np.ascontiguousarray(np.asarray(inputs["W_top2"]).reshape(M1, P, H2).transpose(1, 0, 2))
    a["wt3"] = np.ascontiguousarray(np.asarray(inputs["W_top3"]).reshape(M2, P).T)
    a["b1"] = np.ascontiguousarray(np.asarray(inputs["b_top1"]).reshape(M1, P).T)
    a["b2"] = np.ascontiguousarray(np.asarray(inputs["b_top2"]).reshape(M2, P).T)
    a["ctx_t"] = np.ascontiguousarray(np.asarray(inputs["dense_ctx"]).T)
    one = 0x3F80
    sel = np.zeros((R, SELS, R), np.uint16)
    for col in range(R):
        r, m = divmod(col, NF)
        for part in range(3):
            sel[part * NF + m, 0, col] = one
            for t in range(KT):
                sel[part * NF + (m + RPT * t + r) % NF, 1 + t, col] = one
    c["sel"] = sel
    sel_m = np.zeros((R, NF), np.uint16)
    for row in range(R):
        sel_m[row, row % NF] = one
    c["sel_m"] = sel_m
    own = np.zeros((P, BB), np.float32)
    own[np.arange(P), np.arange(P) // D] = 1
    c["own"] = own
    c["ident"] = np.eye(P, dtype=np.float32)
    c["ident16"] = np.eye(P, dtype=np.uint16) * one
    a.update(c)
    return a


def kernel(**inputs):
    import concourse.bacc as _bacc
    from concourse.bass_utils import run_bass_kernel_spmd as _run

    nc = _bacc.Bacc("TRN2", target_bir_lowering=False, num_devices=1)
    arrays, args = {}, {}
    for name, a in _laid_out(inputs).items():
        arrays[f"in_{name}"] = a
        args[name] = nc.dram_tensor(f"in_{name}", a.shape, mybir.dt.from_np(a.dtype), kind="ExternalInput").ap()
    y = nc.dram_tensor("out_y", (B, 1), F32, kind="ExternalOutput").ap()
    cin_tower(nc, args, y)
    return _run(nc, [arrays], core_ids=[0]).results[0]["out_y"]
```

```python
from contextlib import ExitStack

import concourse.bass as bass
from concourse import mybir

F32 = mybir.dt.float32
F32R = mybir.dt.float32r
BF16 = mybir.dt.bfloat16
I32 = mybir.dt.int32
ALU = mybir.AluOpType
ACT = mybir.ActivationFunctionType

P = 128
B, NF, D, O = 512, 39, 16, 128
CTX, H1, H2 = 16, 512, 256
TILE = 128
TILES = B // TILE
PAIRS = NF * (NF + 1) // 2
KT = -(-PAIRS // P)
REM = PAIRS - (KT - 1) * P
LEAP = 32
LO0 = 2 * LEAP
KROWS = [P] * (KT - 1) + [LO0 + REM]
R = 3 * NF
assert 0 < REM <= LEAP
COLS = 512
GROUPS = TILE * D // COLS
GB = COLS // D
BB = P // D
SUB = GB // BB
MX = NF + 1
PRING = 4
AHEAD = 3
SELS = KT + 1
FIRSTS = (23, 32)
KT_SPAN = 2
SPAN = KT_SPAN * GROUPS
STEPS_FIRST = len(FIRSTS) * SPAN
STEPS0 = KT * GROUPS
assert all(f * (f + 1) // 2 >= (i + 1) * KT_SPAN * P for i, f in enumerate(FIRSTS))
SPLIT_HI, SPLIT_MID, TRANSPOSE, TAKE_T0, TAKE_T1 = 2, 4, 3, 5, 7
PLAIN_EVERY = 6
PLAIN_EARLY = (1, 3)
L2_FIRST = 17
GS = TILES * GROUPS
M1, M2 = H1 // P, H2 // P


PREPS = len(FIRSTS) + TILES


def prep_part(p):
    edges = (0,) + FIRSTS + (NF,)
    return (0, edges[p], edges[p + 1]) if p <= len(FIRSTS) else (p - len(FIRSTS), 0, NF)


def prep_of(t):
    return t + len(FIRSTS)


def step(n):
    return (n % GROUPS, n // GROUPS) if n < STEPS0 else divmod(n, KT)


def steps_of(q):
    return STEPS0 - GROUPS + q + 1 if q < GROUPS else (q + 1) * KT


def plain(n):
    q, k = step(n)
    if k == KT - 1:
        return False
    return n % PLAIN_EVERY == PLAIN_EVERY - 1 if q < GROUPS else early(q) and k in PLAIN_EARLY


def splits(n):
    return sum(not plain(i) for i in range(n + 1))


def left_of(n):
    return n if n < STEPS0 else STEPS0 + n // KT - GROUPS


def left_from(l):
    return l if l < STEPS0 else (l - STEPS0 + GROUPS) * KT


def left_until(l):
    return l + 1 if l < STEPS0 else left_from(l) + KT


SELECTIONS = [entry for n in range(GS * KT)
              for entry in ([("left", left_of(n))] if left_from(left_of(n)) == n else []) + [("right", n)]]


def picks(n):
    end = STEPS0 if n < STEPS0 else GS * KT
    if n < STEPS_FIRST and n % SPAN < TAKE_T1 - 1:
        end = n - n % SPAN + SPAN
    last = min(n + AHEAD, end - 1)
    group_ends = n >= STEPS0 and last + 1 < end and (last + 1) % KT == 0
    return SELECTIONS.index(("right", last)) + 1 + group_ends


def layer2_part(n):
    if n < STEPS0:
        return None
    t, i = n // STEPS0 - 1, n % STEPS0
    if t == 0:
        m0, share = L2_FIRST + 2 * i, 2
    else:
        share = 2 if t < TILES - 2 else 3
        m0 = (i - KT) * share
    return (t, m0, min(m0 + share, NF)) if 0 <= m0 < NF else None


def mlp_tile(q):
    return {GROUPS + 2: 0, 3 * GROUPS: 1, GS - 1: 2}.get(q)


def early(q):
    return q % GROUPS == GROUPS - 1 and GROUPS < q < GS - 1


def turns():
    out = [("z", q, j) for q in range(GROUPS) for j in range(SUB)]
    out += [("parts", prep_of(1), half) for half in range(2)]
    for q in range(GROUPS + 1, GS):
        if early(q):
            out += [("parts", prep_of((q + 1) // GROUPS), half) for half in range(2)]
        out.append(("e", q - 1, 0))
        out += [("z", q - 1, j) for j in range(SUB)]
    return out + [("e", GS - 1, 0)] + [("z", GS - 1, j) for j in range(SUB)]


def cin_tower(nc, A, out):
    ctx = ExitStack()
    with ctx:
        def sb(name, shape, dt=F32):
            return ctx.enter_context(nc.sbuf_tensor(name, shape, dt))

        def sem(name):
            return ctx.enter_context(nc.semaphore(name))

        ident = sb("ident", [P, P])
        ident16 = sb("ident16", [P, P], BF16)
        sel = sb("sel", [R, SELS, P], BF16)
        sel_first = sb("sel_first", [R, 2 * KT, P], BF16)
        sel_m = sb("sel_m", [R, NF], BF16)
        own = sb("own", [P, BB])
        w0 = sb("w0", [P, KT, O])
        w0_hi = sb("w0_hi", [P, KT, O], F32R)
        w0_lo = sb("w0_lo", [P, KT, O], F32R)
        w0_mirror = sb("w0_mirror", [P, KT, O])
        w0f = sb("w0f", [P, KT, O])
        w0f_hi = sb("w0f_hi", [P, KT, O], F32R)
        w0f_lo = sb("w0f_lo", [P, KT, O], F32R)
        w0f_mirror = sb("w0f_mirror", [P, KT, O])
        w1 = sb("w1", [P, NF, O])
        wt1 = sb("wt1", [P, 2, H1])
        wt1_ctx = sb("wt1_ctx", [CTX, H1])
        wt2 = sb("wt2", [P, M1, H2])
        wt3 = sb("wt3", [P, M2])
        b1 = sb("b1", [P, M1])
        b2 = sb("b2", [P, M2])
        ctx_t = sb("ctx_t", [CTX, B])
        ids = sb("ids", [P, TILES, NF], I32)
        emb = sb("emb", [P, TILES, NF * D])
        rest = sb("rest", [P, D, NF])
        parts = sb("parts", [P, D, R], BF16)
        parts_t = [sb(f"parts_t{p}", [R, TILE, D], BF16) for p in range(2)]
        z_sb = [sb(f"z_sb{p}", [P, MX, TILE]) for p in range(2)]
        r2_sb = sb("r2_sb", [P, TILE])
        h1_sb = sb("h1_sb", [P, M1, TILE])
        h2_sb = sb("h2_sb", [P, M2, TILE])
        y_sb = sb("y_sb", [1, B])
        from_ctx = sb("from_ctx", [P, M1, B])
        h1_sum = sb("h1_sum", [P, M1, TILE])
        warm = sb("warm", [1, 1])
        left = [sb(f"left{p}", [P, COLS]) for p in range(2)]
        pairs = [sb(f"pairs{p}", [P, COLS]) for p in range(PRING)]
        pairs_hi = [sb(f"pairs_hi{p}", [P, COLS], F32R) for p in range(PRING)]
        pairs_lo = [sb(f"pairs_lo{p}", [P, COLS], F32R) for p in range(PRING)]
        x1t_sb = [sb(f"x1t_sb{p}", [P, COLS]) for p in range(2)]
        x1_sb = [sb(f"x1_sb{p}", [P, SUB, O]) for p in range(2)]
        diag = [sb(f"diag{p}", [P, SUB, BB, MX]) for p in range(2)]

        bank = [ctx.enter_context(nc.psum_tensor(f"bank{n}", [P, 512], F32)) for n in range(8)]
        ps_sel = bank[0:AHEAD]
        ps_x = bank[3:5]
        ps_mlp = bank[5]
        ps_turn = (bank[7], bank[6])
        ps_last1 = bank[0:M1]
        ps_last2 = bank[4:4 + M2]
        ps_last_y = bank[0]
        turn_order = turns()

        def turn_bank(*entry):
            return ps_turn[turn_order.index(entry) % 2]

        def sel_bank(*entry):
            return ps_sel[SELECTIONS.index(entry) % AHEAD]

        def x_bank(q):
            return (bank[6], bank[5], ps_x[0], ps_x[1])[q] if q < GROUPS else ps_x[q % 2]

        def e_bank(q):
            return ps_sel[q % AHEAD] if q < GROUPS else turn_bank("e", q, 0)

        def parts_bank(p, half):
            if p <= prep_of(0):
                return bank[7] if (p, half) != (0, 0) else bank[6]
            return turn_bank("parts", p, half)

        s_ids = sem("s_ids")
        s_const = sem("s_const")
        s_w0 = sem("s_w0")
        s_w1 = sem("s_w1")
        s_ctx_in = sem("s_ctx_in")
        s_wt = sem("s_wt")
        s_w0_sum = sem("s_w0_sum")
        s_w0_hi = sem("s_w0_hi")
        s_w0_parts = sem("s_w0_parts")
        s_ones = sem("s_ones")
        s_gather = [sem(f"s_gather{p}") for p in range(PREPS)]
        s_zero = sem("s_zero")
        s_hi = sem("s_hi")
        s_rest = sem("s_rest")
        s_mid = sem("s_mid")
        s_parts = sem("s_parts")
        s_pt = sem("s_pt")
        s_parts_t0 = sem("s_parts_t0")
        s_parts_t1 = sem("s_parts_t1")
        s_sel = sem("s_sel")
        s_left = sem("s_left")
        s_pairs = sem("s_pairs")
        s_pairs_hi = sem("s_pairs_hi")
        s_pairs_lo = sem("s_pairs_lo")
        s_l1 = sem("s_l1")
        s_x1t = sem("s_x1t")
        s_xt = sem("s_xt")
        s_x1 = sem("s_x1")
        s_m = sem("s_m")
        s_diag = sem("s_diag")
        s_z = sem("s_z")
        s_z_sb = sem("s_z_sb")
        s_r2 = sem("s_r2")
        s_r2_sb = sem("s_r2_sb")
        s_ctx = sem("s_ctx")
        s_from_ctx = sem("s_from_ctx")
        s_h1_sum = sem("s_h1_sum")
        s_h1 = sem("s_h1")
        s_h1_sb = sem("s_h1_sb")
        s_h2 = sem("s_h2")
        s_h2_sb = sem("s_h2_sb")
        s_y = sem("s_y")
        s_y_sb = sem("s_y_sb")
        s_out = sem("s_out")

        block = ctx.enter_context(nc.Block())

        @block.sync
        def _(sp):
            sp.dma_start(ids[:, :, :], A["ids"].rearrange("(t p) f -> p t f", p=P)).then_inc(s_ids, 16)
            sp.dma_start(wt1_ctx[:, :], A["wt1_ctx"]).then_inc(s_ctx_in, 16)
            sp.dma_start(ctx_t[:, :], A["ctx_t"]).then_inc(s_ctx_in, 16)
            sp.dma_start(b1[:, :], A["b1"]).then_inc(s_ctx_in, 16)
            sp.dma_start(ident16[:, :], A["ident16"].bitcast(BF16)).then_inc(s_const, 16)
            sp.dma_start(ident[:, :], A["ident"]).then_inc(s_const, 16)
            sp.dma_start(sel[:, :, :], A["sel"].bitcast(BF16)).then_inc(s_const, 16)
            sp.dma_start(sel_first[:, :, :], A["sel_first"].bitcast(BF16)).then_inc(s_const, 16)
            sp.dma_start(sel_m[:, :], A["sel_m"].bitcast(BF16)).then_inc(s_const, 16)
            sp.dma_start(own[:, :], A["own"]).then_inc(s_const, 16)
            sp.dma_start(w0f[:, :, :], A["w0f"]).then_inc(s_w0, 16)
            sp.dma_start(w0f_mirror[:, :, :], A["w0f_mirror"]).then_inc(s_w0, 16)
            sp.dma_start(w0[:, :, :], A["w0"]).then_inc(s_w0, 16)
            sp.dma_start(w0_mirror[:, :, :], A["w0_mirror"]).then_inc(s_w0, 16)
            sp.dma_start(w1[:, :, :], A["w1"]).then_inc(s_w1, 16)
            sp.dma_start(wt1[:, :, :], A["wt1"]).then_inc(s_wt, 16)
            sp.dma_start(wt2[:, :, :], A["wt2"]).then_inc(s_wt, 16)
            sp.dma_start(wt3[:, :], A["wt3"]).then_inc(s_wt, 16)
            sp.dma_start(b2[:, :], A["b2"]).then_inc(s_wt, 16)
            sp.wait_ge(s_y_sb, TILES)
            sp.dma_start(out.rearrange("b o -> o b"), y_sb[:, :]).then_inc(s_out, 16)
            sp.wait_ge(s_out, 16)

        @block.gpsimd
        def _(pool):
            pool.wait_ge(s_ids, 16)
            for p in range(PREPS):
                t, f0, f1 = prep_part(p)
                for f in range(f0, f1):
                    nc.gpsimd.indirect_dma_start(
                        out=emb[:, t, f * D:(f + 1) * D], out_offset=None, in_=A[f"tbl_{f}"],
                        in_offset=bass.IndirectOffsetOnAxis(ap=ids[:, t, f:f + 1], axis=0),
                    ).then_inc(s_gather[p], 16)

        @block.scalar
        def _(act):
            def split_hi(p):
                t, f0, f1 = prep_part(p)
                act.wait_ge(s_gather[p], 16 * (f1 - f0))
                if p:
                    act.wait_ge(s_pt, 2 * p)
                nc.scalar.copy(parts[:, :, f0:f1],
                               emb[:, t, f0 * D:f1 * D].rearrange("b (m d) -> b d m", d=D)).then_inc(s_hi, 1)

            def split_mid(p):
                t, f0, f1 = prep_part(p)
                act.wait_ge(s_rest, p + 1)
                nc.scalar.copy(parts[:, :, NF + f0:NF + f1], rest[:, :, f0:f1]).then_inc(s_mid, 1)

            def take_parts_t1(p):
                act.wait_ge(s_pt, 2 * p + 2)
                ps = parts_bank(p, 1)[0:R, :].bitcast(BF16)
                nc.scalar.copy(parts_t[p % 2][:, :, D // 2:D].rearrange("r b d -> r d b"),
                               ps.rearrange("r (d b) -> r d b", b=TILE)).then_inc(s_parts_t1, 1)

            def take_left(l):
                act.wait_ge(s_sel, SELECTIONS.index(("left", l)) + 1)
                if l >= 2:
                    act.wait_ge(s_pairs, left_until(l - 2))
                nc.scalar.copy(left[l % 2][:, :], sel_bank("left", l)[:, :]).then_inc(s_left, 1)

            def pair_hi(n):
                r = KROWS[step(n)[1]]
                if plain(n):
                    return
                act.wait_ge(s_pairs, n + 1)
                if n >= PRING:
                    act.wait_ge(s_l1, n - PRING + 1)
                nc.scalar.copy(pairs_hi[n % PRING][0:r, :], pairs[n % PRING][0:r, :]).then_inc(s_pairs_hi, 1)

            def take_x1t(q):
                act.wait_ge(s_l1, steps_of(q))
                nc.scalar.copy(x1t_sb[q % 2][:, :], x_bank(q)[:, :]).then_inc(s_x1t, 1)

            def take_x1(q):
                act.wait_ge(s_xt, q + 1)
                nc.scalar.copy(x1_sb[q % 2][:, :, :], x_bank(q)[:, :].rearrange("p (j o) -> p j o", j=SUB)).then_inc(s_x1, 1)

            def take_z(q, j):
                act.wait_ge(s_z, q * SUB + j + 1)
                t, g = divmod(q, GROUPS)
                b0 = g * GB + j * BB
                nc.scalar.copy(z_sb[t % 2][:, :, b0:b0 + BB].rearrange("n m b -> n b m"),
                               turn_bank("z", q, j)[:, 0:BB * MX].rearrange("n (b m) -> n b m", m=MX)).then_inc(s_z_sb, 1)

            def take_r2(t):
                act.wait_ge(s_r2, t + 1)
                nc.scalar.copy(r2_sb[:, :], ps_mlp[:, 0:TILE]).then_inc(s_r2_sb, 1)

            def take_h1(t):
                act.wait_ge(s_h1_sum, t + 1)
                nc.scalar.activation(h1_sb[:, :, :], h1_sum[:, :, :], ACT.Relu).then_inc(s_h1_sb, 1)

            def take_h2(t):
                act.wait_ge(s_h2, t + 1)
                for m in range(M2):
                    last = nc.scalar.activation(h2_sb[:, m, :], ps_mlp[:, m * TILE:(m + 1) * TILE], ACT.Relu,
                                                bias=b2[:, m:m + 1])
                last.then_inc(s_h2_sb, 1)

            def take_y(t):
                act.wait_ge(s_y, t + 1)
                nc.scalar.copy(y_sb[:, t * TILE:(t + 1) * TILE], ps_mlp[0:1, 0:TILE]).then_inc(s_y_sb, 1)

            act.wait_ge(s_ids, 16)
            nc.scalar.copy(warm[:, :], ids[0:1, 0, 0:1])
            for m in range(M1):
                act.wait_ge(s_ctx, m + 1)
                act.wait_ge(s_ctx_in, 16 * 3)
                nc.scalar.activation(from_ctx[:, m, :], bank[m][:, :], ACT.Identity,
                                     bias=b1[:, m:m + 1]).then_inc(s_from_ctx, 1)
            act.wait_ge(s_zero, 1)
            hi = 0

            def first_parts(limit):
                nonlocal hi
                while hi < limit:
                    pair_hi(hi)
                    hi += 1

            split_hi(0)
            split_mid(0)
            take_parts_t1(0)
            take_left(0)
            for n in range(STEPS0):
                if n < STEPS_FIRST:
                    p, i = n // SPAN + 1, n % SPAN
                    if i == SPLIT_HI:
                        split_hi(p)
                    if i == SPLIT_MID:
                        split_mid(p)
                    if i == TAKE_T1:
                        take_parts_t1(p)
                if n + 1 < STEPS0:
                    take_left(n + 1)
                first_parts(n + 1)
            take_x1t(0)
            take_x1t(1)
            take_x1(0)
            for q in range(GROUPS):
                if q + 1 < GROUPS:
                    take_x1(q + 1)
                take_z(q, 0)
                take_z(q, 1)
                if q + 2 < GROUPS:
                    take_x1t(q + 2)
                if q == GROUPS - 2:
                    split_hi(prep_of(1))
                take_z(q, 2)
                take_z(q, 3)
                if q == GROUPS - 2:
                    split_mid(prep_of(1))
            take_parts_t1(prep_of(1))
            take_left(STEPS0)
            act.wait_ge(s_wt, 16 * 4)
            for q in range(GROUPS, GS):
                for k in range(KT):
                    n = q * KT + k
                    first_parts(min(n + AHEAD, GS * KT))
                    if k == AHEAD and q < GS - 1:
                        take_left(left_of(n - k + KT))
                    if q > GROUPS:
                        if k == 0:
                            take_x1t(q - 1)
                        if k == 1:
                            if early(q):
                                take_parts_t1(prep_of((q + 1) // GROUPS))
                            take_x1(q - 1)
                        if k >= KT - SUB:
                            take_z(q - 1, k - (KT - SUB))
                    if early(q + 1) and k == KT - 3:
                        split_hi(prep_of((q + 2) // GROUPS))
                    if early(q + 1) and k == KT - 2:
                        split_mid(prep_of((q + 2) // GROUPS))
                    before = layer2_part(n - 1)
                    if before and before[2] == NF:
                        take_r2(before[0])
                    t = mlp_tile(q)
                    if t is not None:
                        if k == 1:
                            take_h1(t)
                        if k == 4:
                            take_h2(t)
                        if k == 6:
                            take_y(t)
            take_x1t(GS - 1)
            take_x1(GS - 1)
            for j in range(SUB):
                take_z(GS - 1, j)
            take_r2(TILES - 1)
            for m in range(M1):
                act.wait_ge(s_h1, TILES + m)
                nc.scalar.activation(h1_sb[:, m, :], ps_last1[m][:, 0:TILE], ACT.Relu,
                                     bias=b1[:, m:m + 1]).then_inc(s_h1_sb, 1)
            for m in range(M2):
                act.wait_ge(s_h2, TILES + m)
                nc.scalar.activation(h2_sb[:, m, :], ps_last2[m][:, 0:TILE], ACT.Relu,
                                     bias=b2[:, m:m + 1]).then_inc(s_h2_sb, 1)
            act.wait_ge(s_y, TILES)
            nc.scalar.copy(y_sb[:, B - TILE:B], ps_last_y[0:1, 0:TILE]).then_inc(s_y_sb, 1)

        @block.vector
        def _(dve):
            def split_rest(p):
                t, f0, f1 = prep_part(p)
                dve.wait_ge(s_hi, p + 1)
                nc.vector.tensor_tensor(rest[:, :, f0:f1], emb[:, t, f0 * D:f1 * D].rearrange("b (m d) -> b d m", d=D),
                                        parts[:, :, f0:f1], ALU.subtract).then_inc(s_rest, 1)

            def split_lo(p):
                t, f0, f1 = prep_part(p)
                dve.wait_ge(s_mid, p + 1)
                dve.wait_ge(s_rest, p + 1)
                nc.vector.tensor_tensor(parts[:, :, 2 * NF + f0:2 * NF + f1], rest[:, :, f0:f1],
                                        parts[:, :, NF + f0:NF + f1], ALU.subtract).then_inc(s_parts, 1)

            def take_parts_t0(p):
                dve.wait_ge(s_pt, 2 * p + 1)
                ps = parts_bank(p, 0)[0:R, :].bitcast(BF16)
                nc.vector.tensor_copy(parts_t[p % 2][:, :, 0:D // 2].rearrange("r b d -> r d b"),
                                      ps.rearrange("r (d b) -> r d b", b=TILE)).then_inc(s_parts_t0, 1)

            def multiply(n):
                r, l = KROWS[step(n)[1]], left_of(n)
                dve.wait_ge(s_sel, SELECTIONS.index(("right", n)) + 1)
                if n == 0 or left_of(n - 1) != l:
                    dve.wait_ge(s_left, l + 1)
                if n >= PRING and plain(n - PRING):
                    dve.wait_ge(s_l1, n - PRING + 1)
                elif n >= PRING:
                    dve.wait_ge(s_pairs_hi, splits(n - PRING))
                    dve.wait_ge(s_pairs_lo, splits(n - PRING))
                nc.vector.tensor_tensor(pairs[n % PRING][0:r, :], sel_bank("right", n)[0:r, :],
                                        left[l % 2][0:r, :], ALU.mult).then_inc(s_pairs, 1)

            def pair_lo(n):
                r = KROWS[step(n)[1]]
                if plain(n):
                    return
                dve.wait_ge(s_pairs_hi, splits(n))
                dve.wait_ge(s_pairs, n + 1)
                if n >= PRING:
                    dve.wait_ge(s_l1, n - PRING + 1)
                r0, to = (LO0, pairs_hi) if r < P else (0, pairs_lo)
                nc.vector.tensor_tensor(to[n % PRING][r0:r, :], pairs[n % PRING][r0:r, :],
                                        pairs_hi[n % PRING][r0:r, :].bitcast(F32), ALU.subtract).then_inc(s_pairs_lo, 1)

            def add_ctx(t):
                dve.wait_ge(s_h1, t + 1)
                nc.vector.tensor_tensor(h1_sum[:, :, :], ps_mlp[:, :].rearrange("p (m b) -> p m b", m=M1),
                                        from_ctx[:, :, t * TILE:(t + 1) * TILE], ALU.add).then_inc(s_h1_sum, 1)

            def spread(q, j):
                if j == 0:
                    dve.wait_ge(s_m, q + 1)
                if q >= 2:
                    dve.wait_ge(s_z, (q - 2) * SUB + j + 1)
                e_m = e_bank(q)[:, j * NF:(j + 1) * NF].unsqueeze(1)
                nc.vector.tensor_tensor(diag[q % 2][:, j, :, 0:NF], e_m.to_broadcast([P, BB, NF]),
                                        own[:, :].unsqueeze(2).to_broadcast([P, BB, NF]),
                                        ALU.mult).then_inc(s_diag, 1)

            nc.vector.memset(parts[:, :, :], 0).then_inc(s_zero, 1)
            dve.wait_ge(s_const, 16 * 6)
            for p in range(2):
                nc.vector.tensor_copy(diag[p][:, :, :, NF:MX],
                                      own[:, :].unsqueeze(1).unsqueeze(3).to_broadcast([P, SUB, BB, 1]),
                                      ).then_inc(s_ones, 1)
            dve.wait_ge(s_w0, 16 * 4)
            for n, (w, mirror, w_hi, w_lo) in enumerate([(w0f, w0f_mirror, w0f_hi, w0f_lo),
                                                         (w0, w0_mirror, w0_hi, w0_lo)]):
                nc.vector.tensor_tensor(w[:, :, :], w[:, :, :], mirror[:, :, :], ALU.add).then_inc(s_w0_sum, 1)
                dve.wait_ge(s_w0_sum, n + 1)
                nc.vector.tensor_copy(w_hi[:, :, :], w[:, :, :]).then_inc(s_w0_hi, 1)
                dve.wait_ge(s_w0_hi, n + 1)
                nc.vector.tensor_tensor(w_lo[:, 0:KT - 1, :], w[:, 0:KT - 1, :], w_hi[:, 0:KT - 1, :].bitcast(F32),
                                        ALU.subtract).then_inc(s_w0_parts, 1)
                nc.vector.tensor_tensor(w_hi[0:REM, KT - 1, :], w[0:REM, KT - 1, :],
                                        w_hi[0:REM, KT - 1, :].bitcast(F32), ALU.subtract).then_inc(s_w0_parts, 1)
            made = low = 0

            def products(limit):
                nonlocal made, low
                while made < limit:
                    multiply(made)
                    made += 1
                    if low < made - 1:
                        pair_lo(low)
                        low += 1
                if made in (STEPS0, GS * KT) and low < made:
                    pair_lo(low)
                    low += 1

            split_rest(0)
            split_lo(0)
            take_parts_t0(0)
            for n in range(STEPS0):
                products(n + 1)
                if n < STEPS_FIRST:
                    p, i = n // SPAN + 1, n % SPAN
                    if i == SPLIT_HI:
                        split_rest(p)
                    if i == SPLIT_MID:
                        split_lo(p)
                    if i == TAKE_T0:
                        take_parts_t0(p)
            for q in range(GROUPS):
                for j in range(SUB):
                    spread(q, j)
            split_rest(prep_of(1))
            split_lo(prep_of(1))
            take_parts_t0(prep_of(1))
            dve.wait_ge(s_from_ctx, M1)
            for q in range(GROUPS, GS):
                for k in range(KT):
                    if k == 1 and mlp_tile(q) is not None:
                        add_ctx(mlp_tile(q))
                    products(min(q * KT + k + AHEAD + 1, GS * KT))
                    if early(q) and k == 0:
                        take_parts_t0(prep_of((q + 1) // GROUPS))
                    if q > GROUPS and 0 <= k - early(q) < 2:
                        for j in range(SUB // 2):
                            spread(q - 1, (k - early(q)) * (SUB // 2) + j)
                    if early(q + 1) and k == KT - 3:
                        split_rest(prep_of((q + 2) // GROUPS))
                    if early(q + 1) and k == KT - 1:
                        split_lo(prep_of((q + 2) // GROUPS))
            for j in range(SUB):
                spread(GS - 1, j)

        @block.tensor
        def _(pe):
            def take_turn(*entry):
                e = turn_order.index(entry)
                if e == 0:
                    pe.wait_ge(s_parts_t1, PREPS - TILES + 1)
                elif e == 1:
                    pe.wait_ge(s_x1, 1)
                else:
                    kind, n, j = turn_order[e - 2]
                    if kind == "parts":
                        pe.wait_ge(s_parts_t1 if j else s_parts_t0, n + 1)
                    elif kind == "e":
                        pe.wait_ge(s_diag, (n + 1) * SUB)
                    else:
                        pe.wait_ge(s_z_sb, n * SUB + j + 1)
                return turn_bank(*entry)

            def transpose_parts(p, half):
                if half == 0:
                    pe.wait_ge(s_parts, p + 1)
                if p > prep_of(0):
                    take_turn("parts", p, half)
                elif p > 0:
                    pe.wait_ge(s_parts_t0 if half else s_parts_t1, p + half)
                ps = parts_bank(p, half)[0:R, :].bitcast(BF16)
                for d in range(D // 2):
                    last = nc.tensor.transpose(ps[:, d * TILE:(d + 1) * TILE],
                                               parts[:, half * (D // 2) + d, :], ident16[:, :])
                last.then_inc(s_pt, 1)

            def select(s):
                side, i = SELECTIONS[s]
                n = i if side == "right" else left_from(i)
                q, k = step(n)
                t, g = divmod(q, GROUPS)
                p = n // SPAN if n < STEPS_FIRST else prep_of(t)
                if side == "left" and (n % SPAN == 0 if n < STEPS_FIRST else g == 0):
                    pe.wait_ge(s_parts_t0, p + 1)
                    pe.wait_ge(s_parts_t1, p + 1)
                if n == STEPS0:
                    pe.wait_ge(s_diag, GROUPS * SUB)
                if s >= AHEAD:
                    before, b = SELECTIONS[s - AHEAD]
                    pe.wait_ge(s_left if before == "left" else s_pairs, b + 1)
                rows = KROWS[k] if side == "right" else P
                if side == "left":
                    pick = sel_first[:, KT + k, :] if n < STEPS0 else sel[:, 0, :]
                else:
                    pick = sel_first[:, k, 0:rows] if t == 0 else sel[:, k + 1, 0:rows]
                nc.tensor.matmul(ps_sel[s % AHEAD][0:rows, :], pick,
                                 parts_t[p % 2][:, g * GB:(g + 1) * GB, :].rearrange("r b d -> r (b d)"),
                                 start=True, stop=True).then_inc(s_sel, 1)

            def layer1(n):
                q, k = step(n)
                r, x = KROWS[k], x_bank(q)[:, :]
                w_hi, w_lo = (w0_hi, w0_lo) if q >= GROUPS else (w0f_hi, w0f_lo)
                if k == 0 and q >= GROUPS:
                    pe.wait_ge(s_x1, q - 1)
                hi, lo = pairs_hi[n % PRING][0:r, :], pairs_lo[n % PRING][0:r, :]
                if plain(n):
                    pe.wait_ge(s_pairs, n + 1)
                    nc.tensor.matmul(x, (w0 if q >= GROUPS else w0f)[0:r, k, :], pairs[n % PRING][0:r, :],
                                     start=(k == 0), stop=False).then_inc(s_l1, 1)
                    return
                pe.wait_ge(s_pairs_hi, splits(n))
                if k == KT - 1:
                    pe.wait_ge(s_pairs_lo, splits(n))
                    nc.tensor.matmul(x, w_hi[0:r, k, :], hi, start=False, stop=True).then_inc(s_l1, 1)
                    return
                nc.tensor.matmul(x, w_lo[0:r, k, :], hi, start=(k == 0), stop=False)
                nc.tensor.matmul(x, w_hi[0:r, k, :], hi, start=False, stop=False)
                pe.wait_ge(s_pairs_lo, splits(n))
                nc.tensor.matmul(x, w_hi[0:r, k, :], lo, start=False, stop=False).then_inc(s_l1, 1)

            def turn_x1(q):
                pe.wait_ge(s_x1t, q + 1)
                for j in range(SUB):
                    last = nc.tensor.transpose(x_bank(q)[:, j * O:(j + 1) * O], x1t_sb[q % 2][:, j * P:(j + 1) * P],
                                               ident[:, :])
                last.then_inc(s_xt, 1)

            def turn_e(q):
                t, g = divmod(q, GROUPS)
                if q < GROUPS:
                    pe.wait_ge(s_pairs, STEPS0)
                    if q >= AHEAD:
                        pe.wait_ge(s_diag, (q - AHEAD + 1) * SUB)
                    ps = e_bank(q)
                else:
                    ps = take_turn("e", q, 0)
                for j in range(SUB):
                    b0 = g * GB + j * BB
                    last = nc.tensor.matmul(ps[:, j * NF:(j + 1) * NF],
                                            parts_t[prep_of(t) % 2][:, b0:b0 + BB, :].rearrange("r b d -> r (b d)"), sel_m[:, :],
                                            start=True, stop=True)
                last.then_inc(s_m, 1)

            def interact(q, j):
                if j == 0:
                    pe.wait_ge(s_x1, q + 1)
                pe.wait_ge(s_diag, q * SUB + j + 1)
                nc.tensor.matmul(take_turn("z", q, j)[:, 0:BB * MX], x1_sb[q % 2][:, j, :],
                                 diag[q % 2][:, j, :, :].rearrange("p b m -> p (b m)"),
                                 start=True, stop=True).then_inc(s_z, 1)

            def layer2(t, m0, m1):
                if m0 == 0:
                    pe.wait_ge(s_z_sb, (t + 1) * (GROUPS * SUB))
                    if t:
                        pe.wait_ge(s_y_sb, t)
                for m in range(m0, m1):
                    last = nc.tensor.matmul(ps_mlp[:, 0:TILE], w1[:, m, :], z_sb[t % 2][:, m, :],
                                            start=(m == 0), stop=(m == NF - 1))
                if m1 == NF:
                    last.then_inc(s_r2, 1)

            def hidden1(t):
                pe.wait_ge(s_r2_sb, t + 1)
                for m in range(M1):
                    o, w = ps_mlp[:, m * TILE:(m + 1) * TILE], slice(m * P, (m + 1) * P)
                    nc.tensor.matmul(o, wt1[:, 0, w], z_sb[t % 2][:, NF, :], start=True, stop=False)
                    last = nc.tensor.matmul(o, wt1[:, 1, w], r2_sb[:, :], start=False, stop=True)
                last.then_inc(s_h1, 1)

            def hidden2(t):
                pe.wait_ge(s_h1_sb, t + 1)
                for m in range(M2):
                    for c in range(M1):
                        last = nc.tensor.matmul(ps_mlp[:, m * TILE:(m + 1) * TILE], wt2[:, c, m * P:(m + 1) * P],
                                                h1_sb[:, c, :], start=(c == 0), stop=(c == M1 - 1))
                last.then_inc(s_h2, 1)

            def output(t):
                pe.wait_ge(s_h2_sb, t + 1)
                for c in range(M2):
                    last = nc.tensor.matmul(ps_mlp[0:1, 0:TILE], wt3[:, c:c + 1], h2_sb[:, c, :],
                                            start=(c == 0), stop=(c == M2 - 1))
                last.then_inc(s_y, 1)

            pe.wait_ge(s_const, 16 * 6)
            pe.wait_ge(s_ones, 2)
            pe.wait_ge(s_ctx_in, 16 * 3)
            for m in range(M1):
                nc.tensor.matmul(bank[m][:, :], wt1_ctx[:, m * P:(m + 1) * P], ctx_t[:, :],
                                 start=True, stop=True).then_inc(s_ctx, 1)
            picked = 0

            def selections(limit):
                nonlocal picked
                while picked < limit:
                    select(picked)
                    picked += 1

            transpose_parts(0, 0)
            transpose_parts(0, 1)
            pe.wait_ge(s_w0_parts, 4)
            pe.wait_ge(s_from_ctx, M1)
            for n in range(STEPS0):
                selections(picks(n))
                layer1(n)
                if n < STEPS_FIRST and n % SPAN in (TRANSPOSE, TRANSPOSE + 1):
                    transpose_parts(n // SPAN + 1, n % SPAN - TRANSPOSE)
            turn_x1(0)
            for q in range(AHEAD):
                turn_e(q)
            for q in range(GROUPS):
                if q + 1 < GROUPS:
                    turn_x1(q + 1)
                for j in range(SUB):
                    interact(q, j)
                if q + AHEAD < GROUPS:
                    turn_e(q + AHEAD)
            pe.wait_ge(s_w1, 16)
            transpose_parts(prep_of(1), 0)
            transpose_parts(prep_of(1), 1)
            layer2(0, 0, L2_FIRST // 3)
            selections(SELECTIONS.index(("left", STEPS0)) + AHEAD)
            layer2(0, L2_FIRST // 3, L2_FIRST)
            pe.wait_ge(s_wt, 16 * 4)
            for q in range(GROUPS, GS):
                for k in range(KT):
                    n = q * KT + k
                    if q > GROUPS and k == early(q):
                        turn_e(q - 1)
                    selections(picks(n))
                    layer1(n)
                    if early(q) and k == 0:
                        transpose_parts(prep_of((q + 1) // GROUPS), 0)
                        transpose_parts(prep_of((q + 1) // GROUPS), 1)
                    if q > GROUPS:
                        if k == 1:
                            turn_x1(q - 1)
                        if k >= KT - SUB:
                            interact(q - 1, k - (KT - SUB))
                    part = layer2_part(n)
                    if part:
                        layer2(*part)
                    t = mlp_tile(q)
                    if t is not None:
                        if k == 0:
                            hidden1(t)
                        if k == 3:
                            hidden2(t)
                        if k == 5:
                            output(t)
            turn_e(GS - 1)
            turn_x1(GS - 1)
            t = TILES - 1
            w1_part = [slice(m * P, (m + 1) * P) for m in range(M1)]
            pe.wait_ge(s_pairs, GS * KT)
            pe.wait_ge(s_x1, GS - 1)
            for m in range(M1):
                nc.tensor.matmul(ps_last1[m][:, 0:TILE], wt1_ctx[:, w1_part[m]], ctx_t[:, t * TILE:B],
                                 start=True, stop=False)
            for j in range(SUB):
                interact(GS - 1, j)
            layer2(t, 0, NF)
            for m in range(M1):
                nc.tensor.matmul(ps_last1[m][:, 0:TILE], wt1[:, 0, w1_part[m]], z_sb[t % 2][:, NF, :],
                                 start=False, stop=False)
            pe.wait_ge(s_r2_sb, TILES)
            for m in range(M1):
                nc.tensor.matmul(ps_last1[m][:, 0:TILE], wt1[:, 1, w1_part[m]], r2_sb[:, :],
                                 start=False, stop=True).then_inc(s_h1, 1)
            for m in range(M2):
                for c in range(M1):
                    if m == 0:
                        pe.wait_ge(s_h1_sb, TILES + c)
                    last = nc.tensor.matmul(ps_last2[m][:, 0:TILE], wt2[:, c, m * P:(m + 1) * P], h1_sb[:, c, :],
                                            start=(c == 0), stop=(c == M1 - 1))
                last.then_inc(s_h2, 1)
            for c in range(M2):
                pe.wait_ge(s_h2_sb, TILES + c)
                last = nc.tensor.matmul(ps_last_y[0:1, 0:TILE], wt3[:, c:c + 1], h2_sb[:, c, :],
                                        start=(c == 0), stop=(c == M2 - 1))
            last.then_inc(s_y, 1)


_TABLES = [f"tbl_{f}" for f in range(NF)]


def _places():
    return ([[(row, k)] for k in range(KT - 1) for row in range(P)]
            + [[(row + LEAP * place, KT - 1) for place in range(3)] for row in range(REM)])


def _left(row):
    low = 3 * LEAP
    return row % LEAP if row < low else LEAP + (row - low) % (NF - LEAP)


_PAIRS = [(m, n) for n in range(NF) for m in range(n + 1)]


def _first_order():
    return {place: pair for pair, places in zip(_PAIRS, _places()) for place in places}


def _shared_order():
    room = [[] for _ in range(NF)]
    for places in _places():
        room[_left(places[0][0])].append(places)
    taken = [[] for _ in range(NF)]

    def put(pair, tried):
        for m in pair:
            if m not in tried:
                tried.add(m)
                if len(taken[m]) < len(room[m]):
                    taken[m].append(pair)
                    return True
                for other in list(taken[m]):
                    if put(other, tried):
                        taken[m].remove(other)
                        taken[m].append(pair)
                        return True
        return False

    for pair in _PAIRS:
        placed = put(pair, set())
        assert placed
    return {place: (left, n if m == left else m) for left in range(NF)
            for (m, n), places in zip(taken[left], room[left]) for place in places}


def _laid_out(inputs):
    import numpy as np

    a = {name: np.ascontiguousarray(inputs[name]) for name in ["ids"] + _TABLES}
    c = {}
    w = np.asarray(inputs["L0_rec_W0"])
    orders = {"w0": _shared_order(), "w0f": _first_order()}
    for name, order in orders.items():
        rows = np.zeros((P, KT, O), w.dtype)
        mirror = np.zeros((P, KT, O), w.dtype)
        for (row, k), (m, n) in order.items():
            rows[row, k] = w[m * NF + n]
            if m != n:
                mirror[row, k] = w[n * NF + m]
        a[name], a[name + "_mirror"] = rows, mirror
    a["w1"] = np.ascontiguousarray(np.asarray(inputs["L0_rec_W1"]).reshape(NF, O, O).transpose(1, 0, 2))
    wt1 = np.asarray(inputs["W_top1"])
    a["wt1"] = np.ascontiguousarray(wt1[:2 * O].reshape(2, P, H1).transpose(1, 0, 2))
    a["wt1_ctx"] = np.ascontiguousarray(wt1[2 * O:])
    a["wt2"] = np.ascontiguousarray(np.asarray(inputs["W_top2"]).reshape(M1, P, H2).transpose(1, 0, 2))
    a["wt3"] = np.ascontiguousarray(np.asarray(inputs["W_top3"]).reshape(M2, P).T)
    a["b1"] = np.ascontiguousarray(np.asarray(inputs["b_top1"]).reshape(M1, P).T)
    a["b2"] = np.ascontiguousarray(np.asarray(inputs["b_top2"]).reshape(M2, P).T)
    a["ctx_t"] = np.ascontiguousarray(np.asarray(inputs["dense_ctx"]).T)
    one = 0x3F80
    sel = np.zeros((R, SELS, P), np.uint16)
    sel_first = np.zeros((R, 2 * KT, P), np.uint16)
    for part in range(3):
        for row in range(P):
            sel[part * NF + _left(row), 0, row] = one
        for (row, k), pair in orders["w0"].items():
            sel[part * NF + pair[1], k + 1, row] = one
        for (row, k), pair in orders["w0f"].items():
            sel_first[part * NF + pair[1], k, row] = one
            sel_first[part * NF + pair[0], KT + k, row] = one
    c["sel"], c["sel_first"] = sel, sel_first
    sel_m = np.zeros((R, NF), np.uint16)
    for row in range(R):
        sel_m[row, row % NF] = one
    c["sel_m"] = sel_m
    own = np.zeros((P, BB), np.float32)
    own[np.arange(P), np.arange(P) // D] = 1
    c["own"] = own
    c["ident"] = np.eye(P, dtype=np.float32)
    c["ident16"] = np.eye(P, dtype=np.uint16) * one
    a.update(c)
    return a


def kernel(**inputs):
    import concourse.bacc as _bacc
    from concourse.bass_utils import run_bass_kernel_spmd as _run

    nc = _bacc.Bacc("TRN2", target_bir_lowering=False, num_devices=1)
    arrays, args = {}, {}
    for name, a in _laid_out(inputs).items():
        arrays[f"in_{name}"] = a
        args[name] = nc.dram_tensor(f"in_{name}", a.shape, mybir.dt.from_np(a.dtype), kind="ExternalInput").ap()
    y = nc.dram_tensor("out_y", (B, 1), F32, kind="ExternalOutput").ap()
    cin_tower(nc, args, y)
    return _run(nc, [arrays], core_ids=[0]).results[0]["out_y"]
```
